# Optimizing a Trainium2 kernel written in Bass

```python
import numpy as np
import jax
import jax.numpy as jnp

def _softmax(x, axis=-1):
    return jax.nn.softmax(x, axis=axis)

def _gelu(x):
    return jax.nn.gelu(x, approximate=True)

def _silu(x):
    return jax.nn.silu(x)

def _sigmoid(x):
    return jax.nn.sigmoid(x)

def _layernorm(x, axis=-1, eps=1e-05):
    m = jnp.mean(x, axis=axis, keepdims=True)
    v = jnp.var(x, axis=axis, keepdims=True)
    return (x - m) / jnp.sqrt(v + eps)

def _scatter_add(tgt, idx, src, axis=0):
    return tgt.at[idx].add(src)

def _segment_sum(src, seg, n):
    return jax.ops.segment_sum(src, seg, n)
kernel_name = 'mk_adj_preln_d1_adj_r2_00ff48'

def setup_inputs(seed: int=0):
    np.random.seed(seed)
    _w = jnp.asarray

    def _rec_inputs():
        import jax
        import jax.numpy as jnp
        _gk = jax.random.key(seed)
        x = 7.22e-05 + 1 * jax.random.normal(jax.random.fold_in(_gk, 1), (4096, 512), jnp.float32)
        _w = (1.0 + jnp.arange(4096, dtype=jnp.float32)) ** (-0.5)
        _w = _w / _w.mean()
        _pij = jnp.clip(0.00390625 * _w[:, None] * _w[None, :], 0.0, 1.0)
        _a = jax.random.uniform(jax.random.fold_in(_gk, 2), (4096, 4096)) < _pij
        _af = _a.astype(jnp.float32)
        adj = _af
        return (x, adj)
    x, adj = _rec_inputs()

    def _L0_gnn_setup():
        import jax, jax.numpy as jnp
        import numpy as np
        N = 4096
        D = 512
        key = jax.random.key(seed)
        ks = jax.random.split(key, 13)
        w_scale = 1.0 / np.sqrt(D)
        inp = {'query': jax.random.normal(ks[0], (N, D), dtype=jnp.float32), 'key': jax.random.normal(ks[1], (N, D), dtype=jnp.float32), 'value': jax.random.normal(ks[2], (N, D), dtype=jnp.float32), 'adj_matrix': jax.random.randint(ks[3], (N, N), 0, 2).astype(jnp.float32), 'Wq': jax.random.normal(ks[4], (D, D), dtype=jnp.float32) * w_scale, 'bq': jax.random.normal(ks[5], (D,), dtype=jnp.float32) * 0.01, 'Wk': jax.random.normal(ks[6], (D, D), dtype=jnp.float32) * w_scale, 'bk': jax.random.normal(ks[7], (D,), dtype=jnp.float32) * 0.01, 'Wv': jax.random.normal(ks[8], (D, D), dtype=jnp.float32) * w_scale, 'bv': jax.random.normal(ks[9], (D,), dtype=jnp.float32) * 0.01, 'Wm': jax.random.normal(ks[10], (D, D), dtype=jnp.float32) * w_scale, 'bm': jax.random.normal(ks[11], (D,), dtype=jnp.float32) * 0.01}
        return inp
    _L0_gnn_all = _L0_gnn_setup()
    _L0_gnn_in = {k: v for k, v in _L0_gnn_all.items() if k in ('key', 'value', 'Wq', 'bq', 'Wk', 'bk', 'Wv', 'bv', 'Wm', 'bm')}
    del _L0_gnn_all
    return {'x': x, 'adj': adj, 'L0_gnn_key': _L0_gnn_in['key'], 'L0_gnn_value': _L0_gnn_in['value'], 'L0_gnn_Wq': _L0_gnn_in['Wq'], 'L0_gnn_bq': _L0_gnn_in['bq'], 'L0_gnn_Wk': _L0_gnn_in['Wk'], 'L0_gnn_bk': _L0_gnn_in['bk'], 'L0_gnn_Wv': _L0_gnn_in['Wv'], 'L0_gnn_bv': _L0_gnn_in['bv'], 'L0_gnn_Wm': _L0_gnn_in['Wm'], 'L0_gnn_bm': _L0_gnn_in['bm']}

def reference(x, adj, L0_gnn_key, L0_gnn_value, L0_gnn_Wq, L0_gnn_bq, L0_gnn_Wk, L0_gnn_bk, L0_gnn_Wv, L0_gnn_bv, L0_gnn_Wm, L0_gnn_bm):
    import jax
    import jax.numpy as jnp

    def _L0_gnn_ref(query, key, value, adj_matrix, Wq, bq, Wk, bk, Wv, bv, Wm, bm):
        import jax, jax.numpy as jnp
        import numpy as np
        N = 4096
        D = 512
        q = query @ Wq.T + bq
        k = key @ Wk.T + bk
        v = value @ Wv.T + bv
        scale = q.shape[0] ** 0.5
        scores = jnp.einsum('nd,md->nm', q, k) / scale
        adj_scores = scores * adj_matrix
        adj_scores = jnp.where(jnp.abs(adj_scores) < 1e-05, -1000000000.0, adj_scores)
        prob = jax.nn.softmax(adj_scores, axis=-1)
        x = jnp.einsum('nm,md->nd', prob, v)
        return x @ Wm.T + bm
    h = jnp.maximum(_layernorm(x, axis=-1), 0.0)
    x = x + _L0_gnn_ref(h, L0_gnn_key, L0_gnn_value, adj, L0_gnn_Wq, L0_gnn_bq, L0_gnn_Wk, L0_gnn_bk, L0_gnn_Wv, L0_gnn_bv, L0_gnn_Wm, L0_gnn_bm)
    return x

_drawn_inputs = setup_inputs


def setup_inputs(seed=0):
    import zlib

    import numpy as np

    out = dict(_drawn_inputs(seed))
    spreads = {}
    factors = {'L0_gnn_bq': 59.222, 'L0_gnn_bk': 64.0, 'L0_gnn_bv': 6.173, 'L0_gnn_bm': 5.768}
    for name, (base, spread) in spreads.items():
        noise = np.random.default_rng([zlib.crc32(name.encode()), seed]).standard_normal(out[name].shape)
        drawn = base * np.exp(spread * noise) if base else spread * noise
        out[name] = jnp.asarray(drawn.astype(out[name].dtype))
    for name, factor in factors.items():
        out[name] = (out[name] * factor).astype(out[name].dtype)
    return out
```

```python
from contextlib import ExitStack

import concourse.bass as bass
from concourse import mybir

ALU = mybir.AluOpType
ACT = mybir.ActivationFunctionType
F32 = mybir.dt.float32
F16 = mybir.dt.float16
BF16 = mybir.dt.bfloat16
U32 = mybir.dt.uint32
AX = mybir.AxisListType
ABSMAX = bass.bass_isa.ReduceOp.absmax

P = 128
N = 4096
D = 512
KC = D // P
TILE = 512
NT = N // TILE
NB = 256
BLOCKS = N // NB
NS = NB // P
CH = 2
STEPS = N // (CH * P)
STEP = CH * NB
RING = STEPS + 2
TOP = 2.0 ** 14
FLOOR = 2.0 ** -60
H_SCALE = 512.0
THRESHOLD = 1e-5
MASKED = -1e9
EPS = 1e-5
NEWTON = 3
LN_STEPS = NS + 8 + 3 * NEWTON
LOG_TOP = 8.25
SCORE_DIV = float(N) ** 0.5
PASSES = ((0, 0), (0, 1), (1, 0))


def after(eng, sem, value):
    if not (isinstance(value, int) and value <= 0):
        eng.wait_ge(sem, value)


def fold_and_project(nc, t, kv_rows, kv_cols, wq, wk, wv, wmT, bq, bk, bv, bm):
    with ExitStack() as ctx:
        sb = lambda name, shape, dt: ctx.enter_context(nc.sbuf_tensor(name, shape, dt))
        sem = lambda name: ctx.enter_context(nc.semaphore(name))

        def borrow(i, n):
            return t.v[:, i * 4096:(i + n) * 4096].bitcast(F32)
        wk_s, wq_s, wv_s, wm_s = (borrow(i, 1).rearrange("p (o d) -> p o d", o=KC) for i in range(4))
        g32, m32 = borrow(4, 1), borrow(5, 1)
        rows = [borrow(6 + s, 1) for s in range(2)]

        cols32 = sb("cols32", [P, 2, KC * TILE], F32)
        cols = sb("cols", [P, 2, 2, KC * TILE], F16)
        gh = sb("gh", [P, 2, KC * D], F16)
        mh = sb("mh", [P, 2, KC * D], F16)
        flat = sb("flat", [P, 2, TILE], F32)
        u_bc = sb("u_bc", [P, D], F32)
        junk = sb("junk", [P, D], F32)
        vecs = sb("vecs", [P, 3, KC], F32)
        wb = sb("wb", [P, KC], F32)
        wb_scaled = sb("wb_scaled", [P, KC], F32)
        craw = sb("craw", [P, N // P], F32)
        bqbk = sb("bqbk", [P, 1], F32)
        tile_max = sb("tile_max", [P, 2 * NT], F32)
        part = sb("part", [P, 8], F32)
        whole = sb("whole", [P, 8], F32)
        pw = sb("pw", [P, 8], F32)
        sc = sb("sc", [P, 16], F32)
        ps = [ctx.enter_context(nc.psum_tensor(f"proj_bank{i}", [P, 512], F32)) for i in range(8)]

        wk_in, wq_in, wv_in, wm_in, vecs_in, bm_in = (sem(s + "_in") for s in ("wk", "wq", "wv", "wm", "vecs", "bm"))
        rows_in = [sem(f"rows_in{s}") for s in range(2)]
        cols_in = [sem(f"cols_in{s}") for s in range(2)]
        rows_used = sem("rows_used")
        folded = sem("folded")
        taken = sem("taken")
        zero_set = sem("zero_set")
        dve_seq = sem("dve_seq")
        key_part = sem("key_part")
        value_part = sem("value_part")
        whole_max = sem("whole_max")
        scales = sem("scales")
        weight_hi = sem("weight_hi")
        weight_lo = sem("weight_lo")
        cols_hi = sem("cols_hi")
        cols_lo = sem("cols_lo")
        bank_ready = sem("bank_ready")
        flat_ready = sem("flat_ready")
        out_hi = sem("out_hi")
        out_lo = sem("out_lo")

        SK, SG, SV, SM, ALPHA_W, ALPHA_V, SIG_W, CSCALE, T0, T1, T2 = range(11)
        col = lambda a, i: a[:, i:i + 1]

        with nc.Block() as block:

            @block.sync
            def _(sp):
                sp.dma_start(vecs[:, 0, :], bq.rearrange("(c p) -> p c", p=P), allow_slow_non_contiguous=True).then_inc(vecs_in, 16)
                sp.dma_start(vecs[:, 1, :], bk.rearrange("(c p) -> p c", p=P), allow_slow_non_contiguous=True).then_inc(vecs_in, 16)
                sp.dma_start(vecs[:, 2, :], bv.rearrange("(c p) -> p c", p=P), allow_slow_non_contiguous=True).then_inc(vecs_in, 16)
                sp.dma_start(wk_s, wk.rearrange("(o p) d -> p o d", p=P)).then_inc(wk_in, 16)
                sp.dma_start(wq_s, wq.rearrange("(o p) d -> p o d", p=P)).then_inc(wq_in, 16)

                def load_rows(i, s):
                    sp.dma_start(rows[s].rearrange("p (r d) -> p r d", r=KC),
                                 kv_rows[bass.ts(i, TILE), :].rearrange("(r p) d -> p r d", p=P)).then_inc(rows_in[s], 16)

                def load_cols(i, s):
                    sp.dma_start(cols32[:, s, :].rearrange("p (e m) -> p e m", e=KC),
                                 kv_cols[:, bass.ts(i, TILE)].rearrange("(e p) m -> p e m", p=P)).then_inc(cols_in[s], 16)

                load_rows(0, 0)
                load_rows(1, 1)
                sp.dma_start(wv_s, wv.rearrange("(o p) d -> p o d", p=P)).then_inc(wv_in, 16)
                sp.dma_start(wm_s, wmT.rearrange("(o p) d -> p o d", p=P)).then_inc(wm_in, 16)
                sp.dma_start(t.out_bias[:, :], bm.partition_broadcast(P)).then_inc(bm_in, 16)
                with sp.Fori(1, NT // 2) as i2:
                    for s in range(2):
                        sp.wait_ge(rows_used, KC * (2 * i2 + s - 1))
                        load_rows(2 * i2 + s, s)
                load_cols(0, 0)
                load_cols(1, 1)
                with sp.Fori(NT // 2, NT) as i2:
                    for s in range(2):
                        sp.wait_ge(rows_used, KC * (2 * i2 + s - 1))
                        load_rows(2 * i2 + s, s)
                        sp.wait_ge(cols_lo, 2 * i2 + s - NT + 1)
                        load_cols(2 * i2 + s - NT + 2, s)
                with sp.Fori(NT // 2 + 1, NT) as i2:
                    for s in range(2):
                        sp.wait_ge(cols_lo, 2 * i2 + s - 1)
                        load_cols(2 * i2 + s, s)

            @block.tensor
            def _(pe):
                def product(bank, w, x):
                    for o in range(KC):
                        last = nc.tensor.matmul(bank, w(o), x(o), start=(o == 0), stop=(o == KC - 1))
                    last.then_inc(folded, 1)

                row = lambda i: (lambda o: vecs[:, i, o:o + 1].to_broadcast([P, P]))
                chunk = lambda a, e: (lambda o: a[:, o, e * P:(e + 1) * P])
                full = lambda a: (lambda o: a[:, o, :])
                colv = lambda i: (lambda o: vecs[:, i, o:o + 1])

                pe.wait_ge(vecs_in, 48)
                pe.wait_ge(wk_in, 16)
                product(ps[4][:, :], row(0), full(wk_s))
                pe.wait_ge(wq_in, 16)
                for e in range(KC):
                    product(ps[e][:, :], chunk(wk_s, e), full(wq_s))
                for d in range(KC):
                    product(ps[5][:, d:d + 1], chunk(wq_s, d), colv(1))
                product(ps[6][:, 0:1], row(0), colv(1))
                pe.wait_ge(wm_in, 16)
                product(ps[7][:, :], row(2), full(wm_s))
                pe.wait_ge(wv_in, 16)
                pe.wait_ge(taken, 5)
                for e in range(KC):
                    product(ps[e][:, :], chunk(wv_s, e), full(wm_s))

                def project(i, s, weights_stay):
                    pe.wait_ge(cols_hi, i + 1)
                    pe.wait_ge(cols_lo, i + 1)
                    for o in range(KC):
                        after(pe, flat_ready, KC * i + o - 7)
                        for n, (e, (a, b)) in enumerate([(e, ab) for e in range(KC) for ab in PASSES]):
                            if weights_stay:
                                l, r = gh[:, a, e * D + o * P:][:, 0:P], cols[:, s, b, e * TILE:(e + 1) * TILE]
                            else:
                                l, r = cols[:, s, a, e * TILE + o * P:][:, 0:P], mh[:, b, e * D:(e + 1) * D]
                            last = nc.tensor.matmul(ps[4 * s + o][:, :], l, r, start=(n == 0), stop=(n == 3 * KC - 1))
                        last.then_inc(bank_ready, 1)

                pe.wait_ge(taken, 12)
                pe.wait_ge(weight_hi, 1)
                pe.wait_ge(weight_lo, 1)
                for s in range(2):
                    project(s, s, True)
                with pe.Fori(1, NT // 2) as i2:
                    for s in range(2):
                        project(2 * i2 + s, s, True)
                pe.wait_ge(weight_hi, 2)
                pe.wait_ge(weight_lo, 2)
                with pe.Fori(NT // 2, NT) as i2:
                    for s in range(2):
                        project(2 * i2 + s, s, False)

            @block.scalar
            def _(act):
                def take(n, out, bank):
                    act.wait_ge(folded, n)
                    nc.scalar.activation(out, bank, ACT.Copy).then_inc(taken, 1)

                take(1, u_bc[:, :], ps[4][:, :])
                for e in range(KC):
                    take(2 + e, g32[:, e * D:(e + 1) * D], ps[e][:, :])
                take(9, wb[:, :], ps[5][:, 0:KC])
                take(10, bqbk[:, :], ps[6][:, 0:1])
                take(11, junk[:, :], ps[7][:, :])
                for e in range(KC):
                    take(12 + e, m32[:, e * D:(e + 1) * D], ps[e][:, :])

                def split(i, s, scale):
                    act.wait_ge(cols_in[s], 16 * (i // 2 + 1) if isinstance(i, int) else 16 * (i >> 1) + 16)
                    if not (isinstance(i, int) and i < 2):
                        act.wait_ge(bank_ready, KC * (i - 1))
                    nc.scalar.activation(cols[:, s, 0, :], cols32[:, s, :], ACT.Copy, scale=col(sc, scale)).then_inc(cols_hi, 1)

                def hi_out(i, value):
                    for o in range(KC):
                        act.wait_ge(flat_ready, KC * i + o + 1)
                        if value:
                            out = t.v[:, bass.ds((i - NT) * (KC * D) + o * D, D)]
                        else:
                            out = t.w[:, bass.ds(i * TILE + o * N, TILE)]
                        nc.scalar.activation(out, flat[:, o % 2, :], ACT.Copy).then_inc(out_hi, 1)

                act.wait_ge(scales, 1)
                nc.scalar.activation(gh[:, 0, :], g32, ACT.Copy, scale=col(sc, SG)).then_inc(weight_hi, 1)
                split(0, 0, SK)
                split(1, 1, SK)
                hi_out(0, False)
                with act.Fori(1, NT // 2) as i2:
                    split(2 * i2, 0, SK)
                    hi_out(2 * i2 - 1, False)
                    split(2 * i2 + 1, 1, SK)
                    hi_out(2 * i2, False)
                act.wait_ge(scales, 2)
                nc.scalar.activation(mh[:, 0, :], m32, ACT.Copy, scale=col(sc, SM)).then_inc(weight_hi, 1)
                split(NT, 0, SV)
                hi_out(NT - 1, False)
                split(NT + 1, 1, SV)
                act.wait_ge(weight_lo, 2)
                hi_out(NT, True)
                with act.Fori(NT // 2 + 1, NT) as i2:
                    split(2 * i2, 0, SV)
                    hi_out(2 * i2 - 1, True)
                    split(2 * i2 + 1, 1, SV)
                    hi_out(2 * i2, True)
                hi_out(2 * NT - 1, True)

            @block.vector
            def _(dve):
                seq = [0]

                def link(ins):
                    seq[0] += 1
                    ins.then_inc(dve_seq, 1)
                    dve.wait_ge(dve_seq, seq[0])

                def row_max(i, s):
                    dve.wait_ge(rows_in[s], 16 * (i // 2 + 1) if isinstance(i, int) else 16 * (i >> 1) + 16)
                    return nc.vector.tensor_reduce(tile_max[:, bass.ds(i, 1)], rows[s], AX.X, ALU.max, apply_absolute_value=True)

                def key_rows(i, s):
                    row_max(i, s)
                    for r in range(KC):
                        after(dve, rows_used, KC * i + r - 1)
                        nc.vector.scalar_tensor_tensor(
                            out=t.p[:, r % 2, :], in0=rows[s][:, r * D:(r + 1) * D], scalar=1.0, in1=u_bc[:, :],
                            op0=ALU.mult, op1=ALU.mult, accum_out=craw[:, bass.ds(KC * i + r, 1)]).then_inc(rows_used, 1)

                dve.wait_ge(taken, 1)
                for s in range(2):
                    key_rows(s, s)
                with dve.Fori(1, NT // 2) as i2:
                    for s in range(2):
                        key_rows(2 * i2 + s, s)

                def power(out, x):
                    link(nc.vector.tensor_scalar(col(pw, T_PW), x, FLOOR, None, ALU.max))
                    link(nc.vector.tensor_scalar(out.bitcast(U32), col(pw, T_PW).bitcast(U32), 0x7F800000, None, ALU.bitwise_and))

                T_PW = 7
                PK, PG, PV_, PM, PW_, = 0, 1, 2, 3, 4
                dve.wait_ge(taken, 12)
                dve.wait_ge(rows_used, KC * NT)
                link(nc.vector.tensor_reduce(col(part, 0), tile_max[:, 0:NT], AX.X, ALU.max))
                link(nc.vector.tensor_reduce(col(part, 1), g32, AX.X, ALU.max, apply_absolute_value=True))
                link(nc.vector.tensor_reduce(col(part, 2), m32, AX.X, ALU.max, apply_absolute_value=True))
                nc.vector.tensor_reduce(col(part, 3), wb[:, :], AX.X, ALU.max, apply_absolute_value=True).then_inc(key_part, 1)
                dve.wait_ge(bm_in, 16)
                nc.vector.tensor_tensor(t.out_bias[:, :], t.out_bias[:, :], junk[:, :], ALU.add)
                dve.wait_ge(whole_max, 1)
                power(col(pw, PK), col(whole, 0))
                power(col(pw, PG), col(whole, 1))
                power(col(pw, PM), col(whole, 2))

                def inverse_scale(out, power_of):
                    link(nc.vector.tensor_scalar(out, power_of, 1.0 / TOP, None, ALU.mult))

                inverse_scale(col(sc, T0), col(pw, PK))
                inverse_scale(col(sc, T1), col(pw, PG))
                link(nc.vector.reciprocal(col(sc, SK), col(sc, T0)))
                link(nc.vector.reciprocal(col(sc, SG), col(sc, T1)))
                link(nc.vector.tensor_scalar(col(sc, T2), col(pw, PK), col(pw, PG), 4.0 * D, ALU.mult, ALU.mult))
                link(nc.vector.tensor_tensor(col(sc, T2), col(sc, T2), col(whole, 3), ALU.add))
                power(col(pw, PW_), col(sc, T2))
                inverse_scale(col(sc, T2), col(pw, PW_))
                link(nc.vector.reciprocal(col(sc, SIG_W), col(sc, T2)))
                link(nc.vector.tensor_tensor(col(sc, ALPHA_W), col(sc, T0), col(sc, T1), ALU.mult))
                link(nc.vector.tensor_tensor(col(sc, ALPHA_W), col(sc, ALPHA_W), col(sc, SIG_W), ALU.mult))
                link(nc.vector.tensor_scalar(wb_scaled[:, :], wb[:, :], col(sc, SIG_W), None, ALU.mult))
                link(nc.vector.tensor_scalar(col(sc, CSCALE), col(sc, SIG_W), H_SCALE, None, ALU.mult))
                link(nc.vector.tensor_scalar(t.c[:, :], craw[:, :], col(bqbk, 0), col(sc, CSCALE), ALU.add, ALU.mult))
                link(nc.vector.tensor_scalar(t.inv_kappa[:, :], col(sc, T2), 1.0 / (H_SCALE * SCORE_DIV), None, ALU.mult))
                link(nc.vector.tensor_scalar(t.threshold[:, :], col(sc, SIG_W), H_SCALE * SCORE_DIV, THRESHOLD, ALU.mult, ALU.mult))
                link(nc.vector.tensor_scalar(t.masked[:, :], col(sc, SIG_W), H_SCALE * SCORE_DIV, MASKED, ALU.mult, ALU.mult))
                nc.vector.memset(t.log_top[:, :], LOG_TOP).then_inc(scales, 1)

                def weight_lo_of(out, x, scale, hi, n):
                    dve.wait_ge(weight_hi, n)
                    nc.vector.scalar_tensor_tensor(out=out, in0=x, scalar=col(sc, scale), in1=hi,
                                                   op0=ALU.mult, op1=ALU.subtract).then_inc(weight_lo, 1)

                def split_lo(i, s, scale):
                    dve.wait_ge(cols_hi, i + 1)
                    nc.vector.scalar_tensor_tensor(out=cols[:, s, 1, :], in0=cols32[:, s, :], scalar=col(sc, scale),
                                                   in1=cols[:, s, 0, :], op0=ALU.mult, op1=ALU.subtract).then_inc(cols_lo, 1)

                def take_out(i, s, value):
                    for o in range(KC):
                        dve.wait_ge(bank_ready, KC * i + o + 1)
                        after(dve, out_lo, KC * i + o - 1)
                        if value:
                            ins = nc.vector.tensor_scalar(flat[:, o % 2, :], ps[4 * s + o][:, :], col(sc, ALPHA_V), None, ALU.mult)
                        else:
                            ins = nc.vector.tensor_scalar(flat[:, o % 2, :], ps[4 * s + o][:, :], col(sc, ALPHA_W),
                                                          wb_scaled[:, o:o + 1], ALU.mult, ALU.add)
                        ins.then_inc(flat_ready, 1)

                weight_lo_of(gh[:, 1, :], g32, SG, gh[:, 0, :], 1)
                split_lo(0, 0, SK)
                split_lo(1, 1, SK)
                row_max(NT, 0).then_inc(rows_used, KC)
                take_out(0, 0, False)
                with dve.Fori(1, NT // 2) as i2:
                    split_lo(2 * i2, 0, SK)
                    row_max(2 * i2 + NT - 1, 1).then_inc(rows_used, KC)
                    take_out(2 * i2 - 1, 1, False)
                    split_lo(2 * i2 + 1, 1, SK)
                    row_max(2 * i2 + NT, 0).then_inc(rows_used, KC)
                    take_out(2 * i2, 0, False)
                row_max(2 * NT - 1, 1).then_inc(rows_used, KC)
                dve.wait_ge(rows_used, KC * 2 * NT)
                nc.vector.tensor_reduce(col(part, 4), tile_max[:, NT:2 * NT], AX.X, ALU.max).then_inc(value_part, 1)
                dve.wait_ge(whole_max, 2)
                power(col(pw, PV_), col(whole, 4))
                inverse_scale(col(sc, T0), col(pw, PV_))
                inverse_scale(col(sc, T1), col(pw, PM))
                link(nc.vector.reciprocal(col(sc, SV), col(sc, T0)))
                link(nc.vector.reciprocal(col(sc, SM), col(sc, T1)))
                link(nc.vector.tensor_scalar(col(sc, T2), col(pw, PV_), col(pw, PM), 4.0 * D, ALU.mult, ALU.mult))
                power(col(pw, PW_), col(sc, T2))
                inverse_scale(t.inv_sigma_v[:, :], col(pw, PW_))
                link(nc.vector.reciprocal(col(sc, T2), t.inv_sigma_v[:, :]))
                link(nc.vector.tensor_tensor(col(sc, ALPHA_V), col(sc, T0), col(sc, T1), ALU.mult))
                nc.vector.tensor_tensor(col(sc, ALPHA_V), col(sc, ALPHA_V), col(sc, T2), ALU.mult).then_inc(scales, 1)
                dve.wait_ge(scales, 2)
                weight_lo_of(mh[:, 1, :], m32, SM, mh[:, 0, :], 2)
                split_lo(NT, 0, SV)
                take_out(NT - 1, 1, False)
                split_lo(NT + 1, 1, SV)
                take_out(NT, 0, True)
                with dve.Fori(NT // 2 + 1, NT) as i2:
                    split_lo(2 * i2, 0, SV)
                    take_out(2 * i2 - 1, 1, True)
                    split_lo(2 * i2 + 1, 1, SV)
                    take_out(2 * i2, 0, True)
                take_out(2 * NT - 1, 1, True)

            @block.gpsimd
            def _(pool):
                nc.gpsimd.memset(t.ident32[:, :], 0.0).then_inc(zero_set, 1)
                pool.wait_ge(zero_set, 1)
                nc.gpsimd.affine_select(out=t.ident32[:, :], in_=t.ident32[:, :], compare_op=ALU.not_equal, fill=1.0,
                                        base=0, pattern=[[-1, P]], channel_multiplier=1).then_inc(zero_set, 1)
                pool.wait_ge(zero_set, 2)
                nc.gpsimd.tensor_copy(t.ident16[:, :], t.ident32[:, :])
                nc.gpsimd.memset(t.ones[:, :], 1.0)
                pool.wait_ge(key_part, 1)
                nc.gpsimd.partition_all_reduce(whole[:, 0:4], part[:, 0:4], P, ABSMAX).then_inc(whole_max, 1)

                def lo_out(i, value):
                    for o in range(KC):
                        pool.wait_ge(out_hi, KC * i + o + 1)
                        if value:
                            hi = t.v[:, bass.ds((i - NT) * (KC * D) + o * D, D)]
                            lo = t.v[:, bass.ds((i - NT) * (KC * D) + o * D + D * N // P, D)]
                        else:
                            hi = t.w[:, bass.ds(i * TILE + o * N, TILE)]
                            lo = t.w[:, bass.ds(i * TILE + (KC + o) * N, TILE)]
                        nc.gpsimd.tensor_tensor(lo, flat[:, o % 2, :], hi, ALU.subtract).then_inc(out_lo, 1)

                with pool.Fori(0, NT - 1) as i:
                    lo_out(i, False)
                pool.wait_ge(value_part, 1)
                nc.gpsimd.partition_all_reduce(whole[:, 4:5], part[:, 4:5], P, ABSMAX).then_inc(whole_max, 1)
                lo_out(NT - 1, False)
                with pool.Fori(NT, 2 * NT) as i:
                    lo_out(i, True)


def attend(nc, t, x, adj_steps, out):
    with ExitStack() as ctx:
        sb = lambda name, shape, dt: ctx.enter_context(nc.sbuf_tensor(name, shape, dt))
        sem = lambda name: ctx.enter_context(nc.semaphore(name))
        pb = lambda name, shape, dt: ctx.enter_context(nc.psum_tensor(name, shape, dt))

        ring = sb("ring", [P, RING * STEP], F32)
        adj = sb("adj", [P, 2, STEP], F32)
        hT = sb("hT", [P, 2 * 2 * KC * NB], F16)
        mask = sb("mask", [P, STEP], F32)
        ph = sb("ph", [P, 2, 2, STEP], F16)
        col_max = sb("col_max", [P, STEP], F32)
        col_sum = sb("col_sum", [P, STEP], F32)
        x_ln = sb("x_ln", [P, NS, D], F32)
        h16 = sb("h16", [P, NS, 2, D], F16)
        x_out = sb("x_out", [P, NS, D], F32)
        stats = sb("stats", [P, NS, 6], F32)
        sums = sb("sums", [P, NS, 2], F32)
        mean = sb("mean", [P, NS], F32)
        var = sb("var", [P, NS], F32)
        newton = sb("newton", [P, NS], F32)
        rstd = sb("rstd", [P, NS], F32)
        max_n = sb("max_n", [P, NS], F32)
        rsum = sb("rsum", [P, NS], F32)

        scores = [pb(f"scores{b}", [P, STEP], F32) for b in range(2)]
        acc = [pb(f"acc{b}", [P, D], F32) for b in range(NS)]
        turned = [pb(f"turned{b}", [P, KC, NB], F16) for b in range(2)]
        max_bank = pb("max_bank", [P, NB], F32)
        row_bank = pb("row_bank", [P, D], F32)

        adj_in = [sem(f"adj_in{s}") for s in range(2)]
        xln_in, xout_in, xout_biased, stored = sem("xln_in"), sem("xout_in"), sem("xout_biased"), sem("stored")
        ln_seq = sem("ln_seq")
        centred, h_hi, h_lo, h_turned, h_ready = sem("centred"), sem("h_hi"), sem("h_lo"), sem("h_turned"), sem("h_ready")
        scores_ready = sem("scores_ready")
        scored = sem("scored")
        magnitude = sem("magnitude")
        mask_ready = sem("mask_ready")
        penalised = sem("penalised")
        maxed = sem("maxed")
        max_folded = sem("max_folded")
        max_turned = sem("max_turned")
        max_found = sem("max_found")
        max_spread = sem("max_spread")
        shifted = sem("shifted")
        exped = sem("exped")
        p_hi, p_lo = sem("p_hi"), sem("p_lo")
        summed = sem("summed")
        multiplied = sem("multiplied")
        rows_summed = sem("rows_summed")
        sum_inv, sum_scaled = sem("sum_inv"), sem("sum_scaled")
        rows_out = sem("rows_out")

        ring_slot = lambda g: ring[:, bass.ts(g % RING, STEP)]
        halves = lambda a: a.rearrange("p (c n) -> p c n", c=CH)

        with nc.Block() as block:

            @block.sync
            def _(sp):
                def load_adj(j, p, s):
                    g = STEPS * j + p
                    after(sp, scored, g - 1)
                    sp.dma_start(adj[:, s, :], adj_steps[bass.ts(g, P), :]).then_inc(adj_in[s], 16)

                def load_x(buf, j, done):
                    sp.dma_start(buf[:, :, :], x[bass.ts(j, NB), :].rearrange("(s p) d -> p s d", p=P)).then_inc(done, 16)

                def store(j):
                    sp.wait_ge(rows_out, j + 1)
                    sp.dma_start(out[bass.ts(j, NB), :].rearrange("(s p) d -> p s d", p=P), x_out[:, :, :]).then_inc(stored, 16)

                def iteration(j):
                    first, second = isinstance(j, int) and j == 0, isinstance(j, int) and j == 1
                    for p in range(4):
                        load_adj(j, p, p % 2)
                    if not (first or second):
                        store(j - 2)
                    with sp.Fori(2, STEPS // 2) as q:
                        for s in range(2):
                            load_adj(j, 2 * q + s, s)
                    if not first:
                        if not second:
                            sp.wait_ge(stored, 16 * (j - 1))
                        load_x(x_out, j - 1, xout_in)
                    if not (isinstance(j, int) and j + 2 >= BLOCKS):
                        sp.wait_ge(h_lo, NS * (j + 2))
                        load_x(x_ln, j + 2, xln_in)

                load_x(x_ln, 0, xln_in)
                sp.wait_ge(h_lo, NS)
                load_x(x_ln, 1, xln_in)
                iteration(0)
                iteration(1)
                with sp.Fori(2, BLOCKS - 2) as j:
                    iteration(j)
                iteration(BLOCKS - 2)
                iteration(BLOCKS - 1)
                store(BLOCKS - 2)
                sp.wait_ge(stored, 16 * (BLOCKS - 1))
                load_x(x_out, BLOCKS - 1, xout_in)
                store(BLOCKS - 1)
                sp.wait_ge(stored, 16 * BLOCKS)

            @block.tensor
            def _(pe):
                def score(j, p, b):
                    g = STEPS * j + p
                    if isinstance(p, int) and p == 0:
                        pe.wait_ge(h_ready, 2 * (j + 1))
                    after(pe, scored, g - 1)
                    for c in range(CH):
                        for n, (d, (a, e)) in enumerate([(d, ab) for d in range(KC) for ab in PASSES]):
                            w = t.w[:, bass.ds((a * KC + d) * N + c * P + p * (CH * P), P)]
                            h = hT[:, bass.ds((j % 2) * (2 * KC * NB) + (e * KC + d) * NB, NB)]
                            last = nc.tensor.matmul(scores[b][:, c * NB:(c + 1) * NB], w, h,
                                                    start=(n == 0), stop=(n == 3 * KC - 1))
                    last.then_inc(scores_ready, 1)

                def times_v(j, p, b):
                    g = STEPS * j + p
                    first, final = isinstance(p, int) and p == 0, isinstance(p, int) and p == STEPS - 1
                    pe.wait_ge(p_hi, g + 1)
                    pe.wait_ge(p_lo, g + 1)
                    if first:
                        after(pe, rows_out, j)
                    for c in range(CH):
                        for s in range(NS):
                            for n, (a, e) in enumerate(PASSES):
                                pr = ph[:, b, a, c * NB + s * P:c * NB + (s + 1) * P]
                                v = t.v[:, bass.ds(e * (D * N // P) + c * D + p * (CH * D), D)]
                                last = nc.tensor.matmul(acc[s][:, :], pr, v, start=first and c == 0 and n == 0,
                                                        stop=final and c == CH - 1 and n == 2)
                    last.then_inc(multiplied, 1)

                def turn_h(k, s):
                    pe.wait_ge(h_hi, NS * k + s + 1)
                    pe.wait_ge(h_lo, NS * k + s + 1)
                    if s == 0:
                        after(pe, h_ready, 2 * k)
                    for a in range(2):
                        for d in range(KC):
                            last = nc.tensor.transpose(turned[a][:, d, s * P:(s + 1) * P],
                                                       h16[:, s, a, d * P:(d + 1) * P], t.ident16[:, :])
                    last.then_inc(h_turned, 1)

                def turn_max(j):
                    pe.wait_ge(max_folded, j + 1)
                    after(pe, sum_inv, j - 1)
                    for s in range(NS):
                        last = nc.tensor.transpose(row_bank[:, s * P:(s + 1) * P], col_max[:, s * P:(s + 1) * P], t.ident32[:, :])
                    last.then_inc(max_turned, 1)

                def spread_max(j):
                    pe.wait_ge(max_found, j + 1)
                    after(pe, shifted, STEPS * j)
                    for s in range(NS):
                        last = nc.tensor.transpose(max_bank[:, s * P:(s + 1) * P], max_n[:, s:s + 1].to_broadcast([P, P]),
                                                   t.ident32[:, :])
                    last.then_inc(max_spread, 1)

                def sum_rows(j):
                    pe.wait_ge(summed, STEPS * (j + 1))
                    pe.wait_ge(max_found, j + 2)
                    for s in range(NS):
                        for c in range(CH):
                            last = nc.tensor.matmul(row_bank[:, s:s + 1], col_sum[:, c * NB + s * P:c * NB + (s + 1) * P],
                                                    t.ones[:, :], start=(c == 0), stop=(c == CH - 1))
                    last.then_inc(rows_summed, 1)

                def iteration(j):
                    fixed = isinstance(j, int)
                    score(j, 0, 0)
                    if not (fixed and j == 0):
                        spread_max(j - 1)
                    if not (fixed and j < 2):
                        sum_rows(j - 2)
                    score(j, 1, 1)
                    if fixed and j == 0:
                        with pe.Fori(1, STEPS // 2) as q:
                            for s in range(2):
                                score(j, 2 * q + s, s)
                    else:
                        for s in range(2):
                            score(j, 2 + s, s)
                            times_v(j - 1, s, s)
                        with pe.Fori(2, STEPS // 2) as q:
                            for s in range(2):
                                score(j, 2 * q + s, s)
                                times_v(j - 1, 2 * q - 2 + s, s)
                    if not (fixed and j == BLOCKS - 1):
                        turn_h(j + 1, 0)
                        turn_h(j + 1, 1)
                    if not (fixed and j == 0):
                        times_v(j - 1, STEPS - 2, 0)
                        times_v(j - 1, STEPS - 1, 1)
                    turn_max(j)

                turn_h(0, 0)
                turn_h(0, 1)
                iteration(0)
                iteration(1)
                with pe.Fori(2, BLOCKS - 1) as j:
                    iteration(j)
                iteration(BLOCKS - 1)
                last_block = BLOCKS - 1
                spread_max(last_block)
                sum_rows(last_block - 1)
                times_v(last_block, 0, 0)
                times_v(last_block, 1, 1)
                with pe.Fori(1, STEPS // 2 - 1) as q:
                    for s in range(2):
                        times_v(last_block, 2 * q + s, s)
                times_v(last_block, STEPS - 2, 0)
                times_v(last_block, STEPS - 1, 1)
                pe.wait_ge(summed, STEPS * BLOCKS)
                for s in range(NS):
                    for c in range(CH):
                        last = nc.tensor.matmul(row_bank[:, s:s + 1], col_sum[:, c * NB + s * P:c * NB + (s + 1) * P],
                                                t.ones[:, :], start=(c == 0), stop=(c == CH - 1))
                last.then_inc(rows_summed, 1)

            @block.vector
            def _(dve):
                def with_adj(j, p, b):
                    g = STEPS * j + p
                    slot = ring_slot(g)
                    dve.wait_ge(scores_ready, g + 1)
                    dve.wait_ge(adj_in[b], 8 * STEPS * j + 8 * (p - b) + 16)
                    for c in range(CH):
                        last = nc.vector.scalar_tensor_tensor(
                            out=slot[:, c * NB:(c + 1) * NB], in0=scores[b][:, c * NB:(c + 1) * NB],
                            scalar=t.c[:, bass.ds(CH * p + c, 1)], in1=adj[:, b, c * NB:(c + 1) * NB],
                            op0=ALU.add, op1=ALU.mult)
                    last.then_inc(scored, 1)

                def mask_scores(j, p):
                    g = STEPS * j + p
                    slot = ring_slot(g)
                    dve.wait_ge(magnitude, g + 1)
                    nc.vector.tensor_scalar(mask[:, :], mask[:, :], t.threshold[:, 0:1], t.masked[:, 0:1],
                                            ALU.is_lt, ALU.mult).then_inc(mask_ready, 1)
                    dve.wait_ge(mask_ready, g + 1)
                    nc.vector.tensor_tensor(slot, mask[:, :], slot, ALU.add).then_inc(penalised, 1)
                    dve.wait_ge(penalised, g + 1)
                    if isinstance(p, int) and p == 0:
                        after(dve, max_turned, j)
                        nc.vector.tensor_scalar(col_max[:, :], slot, 1.0, None, ALU.mult).then_inc(maxed, 1)
                    else:
                        dve.wait_ge(maxed, g)
                        nc.vector.tensor_tensor(col_max[:, :], col_max[:, :], slot, ALU.max).then_inc(maxed, 1)

                def shift(j, p):
                    g = STEPS * j + p
                    slot = halves(ring_slot(g))
                    if isinstance(p, int) and p == 0:
                        dve.wait_ge(max_spread, j + 1)
                    nc.vector.tensor_tensor(slot, slot, max_bank[:, :].unsqueeze(1).to_broadcast([P, CH, NB]),
                                            ALU.subtract).then_inc(shifted, 1)

                def low_half(j, p, b):
                    g = STEPS * j + p
                    dve.wait_ge(p_hi, g + 1)
                    nc.vector.tensor_tensor(ph[:, b, 1, :], t.p[:, b, :], ph[:, b, 0, :], ALU.subtract).then_inc(p_lo, 1)

                def fold_max(j):
                    dve.wait_ge(maxed, STEPS * (j + 1))
                    nc.vector.tensor_tensor(col_max[:, 0:NB], col_max[:, 0:NB], col_max[:, NB:2 * NB], ALU.max).then_inc(max_folded, 1)

                def find_max(j):
                    dve.wait_ge(max_turned, j + 1)
                    nc.vector.tensor_reduce(max_n[:, :], row_bank[:, 0:NB].rearrange("p (s k) -> p s k", s=NS),
                                            AX.X, ALU.max).then_inc(max_found, 1)

                def rows_to_output(j):
                    dve.wait_ge(rows_summed, j + 1)
                    nc.vector.reciprocal(rsum[:, :], row_bank[:, 0:NS]).then_inc(sum_inv, 1)
                    dve.wait_ge(sum_inv, j + 1)
                    nc.vector.tensor_scalar(rsum[:, :], rsum[:, :], t.inv_sigma_v[:, 0:1], None, ALU.mult).then_inc(sum_scaled, 1)
                    dve.wait_ge(sum_scaled, j + 1)
                    dve.wait_ge(multiplied, STEPS * (j + 1))
                    dve.wait_ge(xout_biased, j + 1)
                    for s in range(NS):
                        last = nc.vector.scalar_tensor_tensor(out=x_out[:, s, :], in0=acc[s][:, :], scalar=rsum[:, s:s + 1],
                                                              in1=x_out[:, s, :], op0=ALU.mult, op1=ALU.add)
                    last.then_inc(rows_out, 1)

                def row_statistics(k):
                    done = [LN_STEPS * k]

                    def link(ins):
                        done[0] = done[0] + 1
                        ins.then_inc(ln_seq, 1)
                        dve.wait_ge(ln_seq, done[0])

                    dve.wait_ge(xln_in, 16 * (k + 1))
                    for s in range(NS):
                        link(nc.vector.bn_stats(stats[:, s, :], x_ln[:, s, :]))
                    two = stats[:, :, :].rearrange("p s (e k) -> p s k e", e=2)
                    link(nc.vector.tensor_reduce(sums[:, :, :], two[:, :, 1:3, :], AX.X, ALU.add))
                    link(nc.vector.tensor_tensor(newton[:, :], stats[:, :, 1], stats[:, :, 4], ALU.subtract))
                    link(nc.vector.tensor_scalar(mean[:, :], sums[:, :, 0], 0.5, None, ALU.mult))
                    link(nc.vector.scalar_tensor_tensor(out=newton[:, :], in0=newton[:, :], scalar=0.25, in1=newton[:, :],
                                                        op0=ALU.mult, op1=ALU.mult))
                    link(nc.vector.scalar_tensor_tensor(out=var[:, :], in0=sums[:, :, 1], scalar=1.0 / D, in1=newton[:, :],
                                                        op0=ALU.mult, op1=ALU.add))
                    link(nc.vector.tensor_scalar(var[:, :], var[:, :], EPS, H_SCALE ** -2, ALU.add, ALU.mult))
                    link(nc.vector.tensor_scalar(rstd[:, :].bitcast(U32), var[:, :].bitcast(U32), 1, None, ALU.logical_shift_right))
                    link(nc.vector.tensor_scalar(rstd[:, :].bitcast(U32), rstd[:, :].bitcast(U32), -1.0, float(0x5F3759DF),
                                                 ALU.mult, ALU.add))
                    for _ in range(NEWTON):
                        link(nc.vector.scalar_tensor_tensor(out=newton[:, :], in0=rstd[:, :], scalar=-0.5, in1=rstd[:, :],
                                                            op0=ALU.mult, op1=ALU.mult))
                        link(nc.vector.tensor_tensor(newton[:, :], newton[:, :], var[:, :], ALU.mult))
                        link(nc.vector.scalar_tensor_tensor(out=rstd[:, :], in0=newton[:, :], scalar=1.5, in1=rstd[:, :],
                                                            op0=ALU.add, op1=ALU.mult))

                def layernorm(k, s):
                    n = NS * k + s + 1
                    nc.vector.tensor_scalar(x_ln[:, s, :], x_ln[:, s, :], mean[:, s:s + 1], rstd[:, s:s + 1],
                                            ALU.subtract, ALU.mult).then_inc(centred, 1)
                    dve.wait_ge(h_hi, n)
                    nc.vector.scalar_tensor_tensor(out=h16[:, s, 1, :], in0=x_ln[:, s, :], scalar=0.0, in1=h16[:, s, 0, :],
                                                   op0=ALU.max, op1=ALU.subtract).then_inc(h_lo, 1)

                def both(j, p, b):
                    with_adj(j, p, b)
                    shift(j - 1, p - 1)
                    mask_scores(j, p)
                    low_half(j - 1, p - 1, 1 - b)

                def iteration(j):
                    fixed = isinstance(j, int)
                    before = not (fixed and j == 0)
                    more = not (fixed and j == BLOCKS - 1)
                    if before:
                        find_max(j - 1)
                    with_adj(j, 0, 0)
                    if not (fixed and j < 2):
                        rows_to_output(j - 2)
                    mask_scores(j, 0)

                    def step(p, b):
                        if before:
                            both(j, p, b)
                        else:
                            with_adj(j, p, b)
                            mask_scores(j, p)

                    def pairs(lo, hi):
                        with dve.Fori(lo, hi) as q:
                            step(2 * q, 0)
                            step(2 * q + 1, 1)

                    step(1, 1)
                    pairs(1, 3)
                    if more:
                        row_statistics(j + 1)
                        layernorm(j + 1, 0)
                    pairs(3, 5)
                    if more:
                        layernorm(j + 1, 1)
                    pairs(5, STEPS // 2)
                    fold_max(j)
                    if before:
                        shift(j - 1, STEPS - 1)
                        low_half(j - 1, STEPS - 1, 1)

                row_statistics(0)
                layernorm(0, 0)
                layernorm(0, 1)
                iteration(0)
                iteration(1)
                with dve.Fori(2, BLOCKS - 1) as j:
                    iteration(j)
                iteration(BLOCKS - 1)
                find_max(BLOCKS - 1)
                rows_to_output(BLOCKS - 2)
                for p in range(2):
                    shift(BLOCKS - 1, p)
                    low_half(BLOCKS - 1, p, p)
                with dve.Fori(1, STEPS // 2) as q:
                    for s in range(2):
                        shift(BLOCKS - 1, 2 * q + s)
                        low_half(BLOCKS - 1, 2 * q + s, s)
                rows_to_output(BLOCKS - 1)

            @block.scalar
            def _(act):
                def exps(j, p, b):
                    g = STEPS * j + p
                    act.wait_ge(shifted, g + 1)
                    after(act, p_lo, g - 1)
                    after(act, summed, g - 1)
                    nc.scalar.activation(t.p[:, b, :], ring_slot(g), ACT.Exp, bias=t.log_top[:, 0:1],
                                         scale=t.inv_kappa[:, 0:1]).then_inc(exped, 1)
                    act.wait_ge(exped, g + 1)
                    after(act, multiplied, g - 1)
                    nc.scalar.activation(ph[:, b, 0, :], t.p[:, b, :], ACT.Copy).then_inc(p_hi, 1)

                def magnitudes(j, p):
                    g = STEPS * j + p
                    act.wait_ge(scored, g + 1)
                    after(act, mask_ready, g)
                    after(act, penalised, g)
                    nc.scalar.activation(mask[:, :], ring_slot(g), ACT.Abs).then_inc(magnitude, 1)

                def high_h(k, s):
                    n = NS * k + s + 1
                    act.wait_ge(centred, n)
                    after(act, h_turned, n - NS)
                    nc.scalar.activation(h16[:, s, 0, :], x_ln[:, s, :], ACT.Relu).then_inc(h_hi, 1)

                def take_h(k):
                    act.wait_ge(h_turned, NS * (k + 1))
                    after(act, scores_ready, STEPS * (k - 1))
                    for a in range(2):
                        nc.scalar.activation(hT[:, bass.ds((k % 2) * (2 * KC * NB) + a * (KC * NB), KC * NB)],
                                             turned[a][:, :, :].rearrange("p c n -> p (c n)"), ACT.Copy).then_inc(h_ready, 1)

                def iteration(j):
                    fixed = isinstance(j, int)
                    before = not (fixed and j == 0)
                    more = not (fixed and j == BLOCKS - 1)
                    magnitudes(j, 0)

                    def step(p, b):
                        magnitudes(j, p)
                        if before:
                            exps(j - 1, p - 1, 1 - b)

                    def pairs(lo, hi):
                        with act.Fori(lo, hi) as q:
                            step(2 * q, 0)
                            step(2 * q + 1, 1)

                    step(1, 1)
                    for s in range(2):
                        step(2 + s, s)
                    pairs(2, 3)
                    if more:
                        high_h(j + 1, 0)
                    pairs(3, 5)
                    if more:
                        high_h(j + 1, 1)
                    pairs(5, STEPS // 2)
                    if before:
                        exps(j - 1, STEPS - 1, 1)
                    if more:
                        take_h(j + 1)

                high_h(0, 0)
                high_h(0, 1)
                take_h(0)
                iteration(0)
                iteration(1)
                with act.Fori(2, BLOCKS - 1) as j:
                    iteration(j)
                iteration(BLOCKS - 1)
                with act.Fori(0, STEPS // 2) as q:
                    for s in range(2):
                        exps(BLOCKS - 1, 2 * q + s, s)

            @block.gpsimd
            def _(pool):
                def add_up(j, p, b):
                    g = STEPS * j + p
                    pool.wait_ge(exped, g + 1)
                    if isinstance(p, int) and p == 1:
                        after(pool, rows_summed, j)
                        nc.gpsimd.tensor_tensor(col_sum[:, :], t.p[:, 0, :], t.p[:, 1, :], ALU.add).then_inc(summed, 2)
                    else:
                        pool.wait_ge(summed, g)
                        nc.gpsimd.tensor_tensor(col_sum[:, :], col_sum[:, :], t.p[:, b, :], ALU.add).then_inc(summed, 1)

                def block_sums(j):
                    add_up(j, 1, 1)
                    with pool.Fori(1, STEPS // 2) as q:
                        for s in range(2):
                            add_up(j, 2 * q + s, s)
                    pool.wait_ge(xout_in, 16 * (j + 1))
                    for s in range(NS):
                        last = nc.gpsimd.tensor_tensor(x_out[:, s, :], x_out[:, s, :], t.out_bias[:, :], ALU.add)
                    last.then_inc(xout_biased, 1)

                block_sums(0)
                with pool.Fori(1, BLOCKS) as j:
                    block_sums(j)


class Kept:
    pass


def build(nc, x, adj_steps, kv_rows, kv_cols, wq, wk, wv, wmT, bq, bk, bv, bm, out):
    with ExitStack() as ctx:
        sb = lambda name, shape, dt: ctx.enter_context(nc.sbuf_tensor(name, shape, dt))
        t = Kept()
        t.w = sb("w", [P, 2 * KC * N], F16)
        t.v = sb("v", [P, 2 * (N // P) * D], F16)
        t.p = sb("p", [P, 2, STEP], F32)
        t.out_bias = sb("out_bias", [P, D], F32)
        t.ident32 = sb("ident32", [P, P], F32)
        t.ident16 = sb("ident16", [P, P], F16)
        t.ones = sb("ones", [P, 1], F32)
        t.c = sb("c", [P, N // P], F32)
        column = lambda name: sb(name, [P, 1], F32)
        t.inv_kappa, t.threshold, t.masked = column("inv_kappa"), column("threshold"), column("masked")
        t.log_top, t.inv_sigma_v = column("log_top"), column("inv_sigma_v")
        fold_and_project(nc, t, kv_rows, kv_cols, wq, wk, wv, wmT, bq, bk, bv, bm)
        attend(nc, t, x, adj_steps, out)


def kernel(x, adj, L0_gnn_key, L0_gnn_value, L0_gnn_Wq, L0_gnn_bq, L0_gnn_Wk, L0_gnn_bk, L0_gnn_Wv, L0_gnn_bv,
           L0_gnn_Wm, L0_gnn_bm):
    import numpy as np
    import concourse.bacc as bacc
    from concourse import mybir as mb
    from concourse.bass_utils import run_bass_kernel_spmd

    adj = np.asarray(adj)
    kv = np.concatenate([np.asarray(L0_gnn_key), np.asarray(L0_gnn_value)], axis=0)
    steps = adj.reshape(BLOCKS, NB, STEPS, CH, P).transpose(0, 2, 4, 3, 1).reshape(BLOCKS * STEPS * P, STEP)
    arrays = {
        "x": x, "adj_steps": steps, "kv_rows": kv, "kv_cols": kv.T, "wq": L0_gnn_Wq, "wk": L0_gnn_Wk,
        "wv": L0_gnn_Wv, "wmT": np.asarray(L0_gnn_Wm).T, "bq": L0_gnn_bq, "bk": L0_gnn_bk, "bv": L0_gnn_bv, "bm": L0_gnn_bm,
    }
    arrays = {k: np.ascontiguousarray(a) for k, a in arrays.items()}
    nc = bacc.Bacc("TRN2", target_bir_lowering=False, num_devices=1)
    args = [nc.dram_tensor(k, a.shape, mb.dt.from_np(a.dtype), kind="ExternalInput").ap() for k, a in arrays.items()]
    args.append(nc.dram_tensor("out", (N, D), mb.dt.from_np(np.dtype("float32")), kind="ExternalOutput").ap())
    build(nc, *args)
    r = run_bass_kernel_spmd(nc, [arrays], core_ids=[0])
    return r.results[0]["out"]
```

```python
from contextlib import ExitStack

import concourse.bass as bass
from concourse import mybir

ALU = mybir.AluOpType
ACT = mybir.ActivationFunctionType
F32 = mybir.dt.float32
F16 = mybir.dt.float16
BF16 = mybir.dt.bfloat16
U32 = mybir.dt.uint32
AX = mybir.AxisListType
ABSMAX = bass.bass_isa.ReduceOp.absmax

P = 128
N = 4096
D = 512
KC = D // P
TILE = 512
NT = N // TILE
NB = 256
BLOCKS = N // NB
NS = NB // P
CH = 2
STEPS = N // (CH * P)
STEP = CH * NB
RING = STEPS + 2
TOP = 2.0 ** 14
FLOOR = 2.0 ** -60
H_SCALE = 512.0
THRESHOLD = 1e-5
MASKED = -1e9
EPS = 1e-5
NEWTON = 3
LOG_TOP = 8.25
SCORE_DIV = float(N) ** 0.5
PASSES = ((0, 0), (0, 1), (1, 0))


def after(eng, sem, value):
    if not (isinstance(value, int) and value <= 0):
        eng.wait_ge(sem, value)


def fold_and_project(nc, t, x, kv_rows, kv_cols, wq, wk, wv, wmT, bq, bk, bv, bm):
    with ExitStack() as ctx:
        sb = lambda name, shape, dt: ctx.enter_context(nc.sbuf_tensor(name, shape, dt))
        sem = lambda name: ctx.enter_context(nc.semaphore(name))

        def borrow(i, n):
            return t.v[:, i * 4096:(i + n) * 4096].bitcast(F32)
        wk_s, wq_s, wv_s, wm_s = (borrow(i, 1).rearrange("p (o d) -> p o d", o=KC) for i in range(4))
        g32, m32 = borrow(4, 1), borrow(5, 1)
        rows = [borrow(6 + s, 1) for s in range(2)]

        cols32 = sb("cols32", [P, 2, KC * TILE], F32)
        cols = sb("cols", [P, 2, 2, KC * TILE], F16)
        gh = sb("gh", [P, 2, KC * D], F16)
        mh = sb("mh", [P, 2, KC * D], F16)
        flat = sb("flat", [P, 2, TILE], F32)
        u_bc = sb("u_bc", [P, D], F32)
        x_rows = sb("x_rows", [P, 2, KC * D], F32)
        stats = sb("stats", [P, N // P, 6], F32)
        vecs = sb("vecs", [P, 3, KC], F32)
        wb = sb("wb", [P, KC], F32)
        wb_scaled = sb("wb_scaled", [P, KC], F32)
        craw = sb("craw", [P, N // P], F32)
        bqbk = sb("bqbk", [P, 1], F32)
        tile_max = sb("tile_max", [P, 2 * NT], F32)
        var = sb("var", [P, N // P], F32)
        newton = sb("newton", [P, N // P], F32)
        part = sb("part", [P, 8], F32)
        whole = sb("whole", [P, 8], F32)
        pw = sb("pw", [P, 8], F32)
        sc = sb("sc", [P, 16], F32)
        ps = [ctx.enter_context(nc.psum_tensor(f"proj_bank{i}", [P, 512], F32)) for i in range(8)]

        wk_in, wq_in, wv_in, wm_in, vecs_in, bm_in = (sem(s + "_in") for s in ("wk", "wq", "wv", "wm", "vecs", "bm"))
        rows_in = [sem(f"rows_in{s}") for s in range(2)]
        cols_in = [sem(f"cols_in{s}") for s in range(2)]
        x_in = [sem(f"x_in{s}") for s in range(2)]
        x_used = sem("x_used")
        rows_used = sem("rows_used")
        folded = sem("folded")
        taken = sem("taken")
        zero_set = sem("zero_set")
        dve_seq = sem("dve_seq")
        key_part = sem("key_part")
        value_part = sem("value_part")
        whole_max = sem("whole_max")
        scales = sem("scales")
        weight_hi = sem("weight_hi")
        weight_lo = sem("weight_lo")
        cols_hi = sem("cols_hi")
        cols_lo = sem("cols_lo")
        bank_ready = sem("bank_ready")
        flat_ready = sem("flat_ready")
        out_hi = sem("out_hi")
        out_lo = sem("out_lo")

        SK, SG, SV, SM, ALPHA_W, ALPHA_V, SIG_W, CSCALE, T0, T1, T2 = range(11)
        col = lambda a, i: a[:, i:i + 1]

        with nc.Block() as block:

            @block.sync
            def _(sp):
                sp.dma_start(vecs[:, 0, :], bq.rearrange("(c p) -> p c", p=P), allow_slow_non_contiguous=True).then_inc(vecs_in, 16)
                sp.dma_start(vecs[:, 1, :], bk.rearrange("(c p) -> p c", p=P), allow_slow_non_contiguous=True).then_inc(vecs_in, 16)
                sp.dma_start(vecs[:, 2, :], bv.rearrange("(c p) -> p c", p=P), allow_slow_non_contiguous=True).then_inc(vecs_in, 16)
                sp.dma_start(wk_s, wk.rearrange("(o p) d -> p o d", p=P)).then_inc(wk_in, 16)
                sp.dma_start(wq_s, wq.rearrange("(o p) d -> p o d", p=P)).then_inc(wq_in, 16)

                def load_rows(i, s):
                    sp.dma_start(rows[s].rearrange("p (r d) -> p r d", r=KC),
                                 kv_rows[bass.ts(i, TILE), :].rearrange("(r p) d -> p r d", p=P)).then_inc(rows_in[s], 16)

                def load_cols(i, s):
                    sp.dma_start(cols32[:, s, :].rearrange("p (e m) -> p e m", e=KC),
                                 kv_cols[:, bass.ts(i, TILE)].rearrange("(e p) m -> p e m", p=P)).then_inc(cols_in[s], 16)

                load_rows(0, 0)
                load_rows(1, 1)
                sp.dma_start(wv_s, wv.rearrange("(o p) d -> p o d", p=P)).then_inc(wv_in, 16)
                sp.dma_start(wm_s, wmT.rearrange("(o p) d -> p o d", p=P)).then_inc(wm_in, 16)
                sp.dma_start(t.out_bias[:, :], bm.partition_broadcast(P)).then_inc(bm_in, 16)
                with sp.Fori(1, NT // 2) as i2:
                    for s in range(2):
                        sp.wait_ge(rows_used, KC * (2 * i2 + s - 1))
                        load_rows(2 * i2 + s, s)
                load_cols(0, 0)
                load_cols(1, 1)
                with sp.Fori(NT // 2, NT) as i2:
                    for s in range(2):
                        sp.wait_ge(rows_used, KC * (2 * i2 + s - 1))
                        load_rows(2 * i2 + s, s)
                        sp.wait_ge(cols_lo, 2 * i2 + s - NT + 1)
                        load_cols(2 * i2 + s - NT + 2, s)

                def load_x(i, s):
                    sp.dma_start(x_rows[:, s, :].rearrange("p (r d) -> p r d", r=KC),
                                 x[bass.ts(i, TILE), :].rearrange("(r p) d -> p r d", p=P)).then_inc(x_in[s], 16)

                load_x(0, 0)
                load_x(1, 1)
                with sp.Fori(NT // 2 + 1, NT) as i2:
                    for s in range(2):
                        sp.wait_ge(cols_lo, 2 * i2 + s - 1)
                        load_cols(2 * i2 + s, s)
                        sp.wait_ge(x_used, KC * (2 * i2 + s - NT - 1))
                        load_x(2 * i2 + s - NT, s)

            @block.tensor
            def _(pe):
                def product(bank, w, x):
                    for o in range(KC):
                        last = nc.tensor.matmul(bank, w(o), x(o), start=(o == 0), stop=(o == KC - 1))
                    last.then_inc(folded, 1)

                row = lambda i: (lambda o: vecs[:, i, o:o + 1].to_broadcast([P, P]))
                chunk = lambda a, e: (lambda o: a[:, o, e * P:(e + 1) * P])
                full = lambda a: (lambda o: a[:, o, :])
                colv = lambda i: (lambda o: vecs[:, i, o:o + 1])

                pe.wait_ge(vecs_in, 48)
                pe.wait_ge(wk_in, 16)
                product(ps[4][:, :], row(0), full(wk_s))
                pe.wait_ge(wq_in, 16)
                for e in range(KC):
                    product(ps[e][:, :], chunk(wk_s, e), full(wq_s))
                for d in range(KC):
                    product(ps[5][:, d:d + 1], chunk(wq_s, d), colv(1))
                product(ps[6][:, 0:1], row(0), colv(1))
                pe.wait_ge(wm_in, 16)
                product(ps[7][:, :], row(2), full(wm_s))
                pe.wait_ge(wv_in, 16)
                pe.wait_ge(taken, 5)
                for e in range(KC):
                    product(ps[e][:, :], chunk(wv_s, e), full(wm_s))

                def project(i, s, weights_stay):
                    pe.wait_ge(cols_hi, i + 1)
                    pe.wait_ge(cols_lo, i + 1)
                    for o in range(KC):
                        after(pe, flat_ready, KC * i + o - 7)
                        for n, (e, (a, b)) in enumerate([(e, ab) for e in range(KC) for ab in PASSES]):
                            if weights_stay:
                                l, r = gh[:, a, e * D + o * P:][:, 0:P], cols[:, s, b, e * TILE:(e + 1) * TILE]
                            else:
                                l, r = cols[:, s, a, e * TILE + o * P:][:, 0:P], mh[:, b, e * D:(e + 1) * D]
                            last = nc.tensor.matmul(ps[4 * s + o][:, :], l, r, start=(n == 0), stop=(n == 3 * KC - 1))
                        last.then_inc(bank_ready, 1)

                pe.wait_ge(taken, 11)
                pe.wait_ge(weight_hi, 1)
                pe.wait_ge(weight_lo, 1)
                for s in range(2):
                    project(s, s, True)
                with pe.Fori(1, NT // 2) as i2:
                    for s in range(2):
                        project(2 * i2 + s, s, True)
                pe.wait_ge(weight_hi, 2)
                pe.wait_ge(weight_lo, 2)
                with pe.Fori(NT // 2, NT) as i2:
                    for s in range(2):
                        project(2 * i2 + s, s, False)

            @block.scalar
            def _(act):
                def take(n, out, bank):
                    act.wait_ge(folded, n)
                    nc.scalar.activation(out, bank, ACT.Copy).then_inc(taken, 1)

                take(1, u_bc[:, :], ps[4][:, :])
                for e in range(KC):
                    take(2 + e, g32[:, e * D:(e + 1) * D], ps[e][:, :])
                take(9, wb[:, :], ps[5][:, 0:KC])
                take(10, bqbk[:, :], ps[6][:, 0:1])
                for e in range(KC):
                    take(12 + e, m32[:, e * D:(e + 1) * D], ps[e][:, :])

                def split(i, s, scale):
                    act.wait_ge(cols_in[s], 16 * (i // 2 + 1) if isinstance(i, int) else 16 * (i >> 1) + 16)
                    if not (isinstance(i, int) and i < 2):
                        act.wait_ge(bank_ready, KC * (i - 1))
                    nc.scalar.activation(cols[:, s, 0, :], cols32[:, s, :], ACT.Copy, scale=col(sc, scale)).then_inc(cols_hi, 1)

                def hi_out(i, value):
                    for o in range(KC):
                        act.wait_ge(flat_ready, KC * i + o + 1)
                        if value:
                            out = t.v[:, bass.ds((i - NT) * (KC * D) + o * D, D)]
                        else:
                            out = t.w[:, bass.ds(i * TILE + o * N, TILE)]
                        nc.scalar.activation(out, flat[:, o % 2, :], ACT.Copy).then_inc(out_hi, 1)

                act.wait_ge(scales, 1)
                nc.scalar.activation(gh[:, 0, :], g32, ACT.Copy, scale=col(sc, SG)).then_inc(weight_hi, 1)
                split(0, 0, SK)
                split(1, 1, SK)
                hi_out(0, False)
                with act.Fori(1, NT // 2) as i2:
                    split(2 * i2, 0, SK)
                    hi_out(2 * i2 - 1, False)
                    split(2 * i2 + 1, 1, SK)
                    hi_out(2 * i2, False)
                act.wait_ge(scales, 2)
                nc.scalar.activation(mh[:, 0, :], m32, ACT.Copy, scale=col(sc, SM)).then_inc(weight_hi, 1)
                split(NT, 0, SV)
                hi_out(NT - 1, False)
                split(NT + 1, 1, SV)
                act.wait_ge(weight_lo, 2)
                hi_out(NT, True)
                with act.Fori(NT // 2 + 1, NT) as i2:
                    split(2 * i2, 0, SV)
                    hi_out(2 * i2 - 1, True)
                    split(2 * i2 + 1, 1, SV)
                    hi_out(2 * i2, True)
                hi_out(2 * NT - 1, True)

            @block.vector
            def _(dve):
                seq = [0]

                def link(ins):
                    seq[0] += 1
                    ins.then_inc(dve_seq, 1)
                    dve.wait_ge(dve_seq, seq[0])

                def row_max(i, s):
                    dve.wait_ge(rows_in[s], 16 * (i // 2 + 1) if isinstance(i, int) else 16 * (i >> 1) + 16)
                    return nc.vector.tensor_reduce(tile_max[:, bass.ds(i, 1)], rows[s], AX.X, ALU.max, apply_absolute_value=True)

                def key_rows(i, s):
                    row_max(i, s)
                    for r in range(KC):
                        after(dve, rows_used, KC * i + r - 1)
                        nc.vector.scalar_tensor_tensor(
                            out=t.p[:, r % 2, :], in0=rows[s][:, r * D:(r + 1) * D], scalar=1.0, in1=u_bc[:, :],
                            op0=ALU.mult, op1=ALU.mult, accum_out=craw[:, bass.ds(KC * i + r, 1)]).then_inc(rows_used, 1)

                dve.wait_ge(taken, 1)
                for s in range(2):
                    key_rows(s, s)
                with dve.Fori(1, NT // 2) as i2:
                    for s in range(2):
                        key_rows(2 * i2 + s, s)

                def power(out, x):
                    link(nc.vector.tensor_scalar(col(pw, T_PW), x, FLOOR, None, ALU.max))
                    link(nc.vector.tensor_scalar(out.bitcast(U32), col(pw, T_PW).bitcast(U32), 0x7F800000, None, ALU.bitwise_and))

                T_PW = 7
                PK, PG, PV_, PM, PW_, = 0, 1, 2, 3, 4
                dve.wait_ge(taken, 11)
                dve.wait_ge(rows_used, KC * NT)
                link(nc.vector.tensor_reduce(col(part, 0), tile_max[:, 0:NT], AX.X, ALU.max))
                link(nc.vector.tensor_reduce(col(part, 1), g32, AX.X, ALU.max, apply_absolute_value=True))
                link(nc.vector.tensor_reduce(col(part, 2), m32, AX.X, ALU.max, apply_absolute_value=True))
                nc.vector.tensor_reduce(col(part, 3), wb[:, :], AX.X, ALU.max, apply_absolute_value=True).then_inc(key_part, 1)
                dve.wait_ge(bm_in, 16)
                dve.wait_ge(folded, 11)
                nc.vector.tensor_tensor(t.out_bias[:, :], t.out_bias[:, :], ps[7][:, :], ALU.add)
                dve.wait_ge(whole_max, 1)
                power(col(pw, PK), col(whole, 0))
                power(col(pw, PG), col(whole, 1))
                power(col(pw, PM), col(whole, 2))

                def inverse_scale(out, power_of):
                    link(nc.vector.tensor_scalar(out, power_of, 1.0 / TOP, None, ALU.mult))

                inverse_scale(col(sc, T0), col(pw, PK))
                inverse_scale(col(sc, T1), col(pw, PG))
                link(nc.vector.reciprocal(col(sc, SK), col(sc, T0)))
                link(nc.vector.reciprocal(col(sc, SG), col(sc, T1)))
                link(nc.vector.tensor_scalar(col(sc, T2), col(pw, PK), col(pw, PG), 4.0 * D, ALU.mult, ALU.mult))
                link(nc.vector.tensor_tensor(col(sc, T2), col(sc, T2), col(whole, 3), ALU.add))
                power(col(pw, PW_), col(sc, T2))
                inverse_scale(col(sc, T2), col(pw, PW_))
                link(nc.vector.reciprocal(col(sc, SIG_W), col(sc, T2)))
                link(nc.vector.tensor_tensor(col(sc, ALPHA_W), col(sc, T0), col(sc, T1), ALU.mult))
                link(nc.vector.tensor_tensor(col(sc, ALPHA_W), col(sc, ALPHA_W), col(sc, SIG_W), ALU.mult))
                link(nc.vector.tensor_scalar(wb_scaled[:, :], wb[:, :], col(sc, SIG_W), None, ALU.mult))
                link(nc.vector.tensor_scalar(col(sc, CSCALE), col(sc, SIG_W), H_SCALE, None, ALU.mult))
                link(nc.vector.tensor_scalar(t.c[:, :], craw[:, :], col(bqbk, 0), col(sc, CSCALE), ALU.add, ALU.mult))
                link(nc.vector.tensor_scalar(t.inv_kappa[:, :], col(sc, T2), 1.0 / (H_SCALE * SCORE_DIV), None, ALU.mult))
                link(nc.vector.tensor_scalar(t.threshold[:, :], col(sc, SIG_W), H_SCALE * SCORE_DIV, THRESHOLD, ALU.mult, ALU.mult))
                link(nc.vector.tensor_scalar(t.masked[:, :], col(sc, SIG_W), H_SCALE * SCORE_DIV, MASKED, ALU.mult, ALU.mult))
                nc.vector.memset(t.log_top[:, :], LOG_TOP).then_inc(scales, 1)

                def weight_lo_of(out, x, scale, hi, n):
                    dve.wait_ge(weight_hi, n)
                    nc.vector.scalar_tensor_tensor(out=out, in0=x, scalar=col(sc, scale), in1=hi,
                                                   op0=ALU.mult, op1=ALU.subtract).then_inc(weight_lo, 1)

                def split_lo(i, s, scale):
                    dve.wait_ge(cols_hi, i + 1)
                    nc.vector.scalar_tensor_tensor(out=cols[:, s, 1, :], in0=cols32[:, s, :], scalar=col(sc, scale),
                                                   in1=cols[:, s, 0, :], op0=ALU.mult, op1=ALU.subtract).then_inc(cols_lo, 1)

                def take_out(i, s, value):
                    for o in range(KC):
                        dve.wait_ge(bank_ready, KC * i + o + 1)
                        after(dve, out_lo, KC * i + o - 1)
                        if value:
                            ins = nc.vector.tensor_scalar(flat[:, o % 2, :], ps[4 * s + o][:, :], col(sc, ALPHA_V), None, ALU.mult)
                        else:
                            ins = nc.vector.tensor_scalar(flat[:, o % 2, :], ps[4 * s + o][:, :], col(sc, ALPHA_W),
                                                          wb_scaled[:, o:o + 1], ALU.mult, ALU.add)
                        ins.then_inc(flat_ready, 1)

                weight_lo_of(gh[:, 1, :], g32, SG, gh[:, 0, :], 1)
                split_lo(0, 0, SK)
                split_lo(1, 1, SK)
                row_max(NT, 0).then_inc(rows_used, KC)
                take_out(0, 0, False)
                with dve.Fori(1, NT // 2) as i2:
                    split_lo(2 * i2, 0, SK)
                    row_max(2 * i2 + NT - 1, 1).then_inc(rows_used, KC)
                    take_out(2 * i2 - 1, 1, False)
                    split_lo(2 * i2 + 1, 1, SK)
                    row_max(2 * i2 + NT, 0).then_inc(rows_used, KC)
                    take_out(2 * i2, 0, False)
                row_max(2 * NT - 1, 1).then_inc(rows_used, KC)
                dve.wait_ge(rows_used, KC * 2 * NT)
                nc.vector.tensor_reduce(col(part, 4), tile_max[:, NT:2 * NT], AX.X, ALU.max).then_inc(value_part, 1)
                dve.wait_ge(whole_max, 2)
                power(col(pw, PV_), col(whole, 4))
                inverse_scale(col(sc, T0), col(pw, PV_))
                inverse_scale(col(sc, T1), col(pw, PM))
                link(nc.vector.reciprocal(col(sc, SV), col(sc, T0)))
                link(nc.vector.reciprocal(col(sc, SM), col(sc, T1)))
                link(nc.vector.tensor_scalar(col(sc, T2), col(pw, PV_), col(pw, PM), 4.0 * D, ALU.mult, ALU.mult))
                power(col(pw, PW_), col(sc, T2))
                inverse_scale(t.inv_sigma_v[:, :], col(pw, PW_))
                link(nc.vector.reciprocal(col(sc, T2), t.inv_sigma_v[:, :]))
                link(nc.vector.tensor_tensor(col(sc, ALPHA_V), col(sc, T0), col(sc, T1), ALU.mult))
                nc.vector.tensor_tensor(col(sc, ALPHA_V), col(sc, ALPHA_V), col(sc, T2), ALU.mult).then_inc(scales, 1)
                dve.wait_ge(scales, 2)
                weight_lo_of(mh[:, 1, :], m32, SM, mh[:, 0, :], 2)

                def x_stats(i, s):
                    dve.wait_ge(x_in[s], 16 * (i // 2 + 1) if isinstance(i, int) else 16 * (i >> 1) + 16)
                    for r in range(KC):
                        nc.vector.bn_stats(stats[:, bass.ds(KC * i + r, 1), :].rearrange("p o k -> p (o k)"),
                                           x_rows[:, s, r * D:(r + 1) * D]).then_inc(x_used, 1)

                split_lo(NT, 0, SV)
                take_out(NT - 1, 1, False)
                x_stats(0, 0)
                split_lo(NT + 1, 1, SV)
                take_out(NT, 0, True)
                x_stats(1, 1)
                with dve.Fori(NT // 2 + 1, NT) as i2:
                    split_lo(2 * i2, 0, SV)
                    take_out(2 * i2 - 1, 1, True)
                    x_stats(2 * i2 - NT, 0)
                    split_lo(2 * i2 + 1, 1, SV)
                    take_out(2 * i2, 0, True)
                    x_stats(2 * i2 + 1 - NT, 1)
                take_out(2 * NT - 1, 1, True)

                dve.wait_ge(x_used, KC * NT)
                link(nc.vector.tensor_tensor(t.mean[:, :], stats[:, :, 1], stats[:, :, 4], ALU.add))
                link(nc.vector.tensor_tensor(newton[:, :], stats[:, :, 1], stats[:, :, 4], ALU.subtract))
                link(nc.vector.tensor_tensor(var[:, :], stats[:, :, 2], stats[:, :, 5], ALU.add))
                link(nc.vector.tensor_scalar(t.mean[:, :], t.mean[:, :], 0.5, None, ALU.mult))
                link(nc.vector.scalar_tensor_tensor(out=newton[:, :], in0=newton[:, :], scalar=0.25, in1=newton[:, :],
                                                    op0=ALU.mult, op1=ALU.mult))
                link(nc.vector.scalar_tensor_tensor(out=var[:, :], in0=var[:, :], scalar=1.0 / D, in1=newton[:, :],
                                                    op0=ALU.mult, op1=ALU.add))
                link(nc.vector.tensor_scalar(var[:, :], var[:, :], EPS, H_SCALE ** -2, ALU.add, ALU.mult))
                link(nc.vector.tensor_scalar(t.rstd[:, :].bitcast(U32), var[:, :].bitcast(U32), 1, None, ALU.logical_shift_right))
                link(nc.vector.tensor_scalar(t.rstd[:, :].bitcast(U32), t.rstd[:, :].bitcast(U32), -1.0, float(0x5F3759DF),
                                             ALU.mult, ALU.add))
                for _ in range(NEWTON):
                    link(nc.vector.scalar_tensor_tensor(out=newton[:, :], in0=t.rstd[:, :], scalar=-0.5, in1=t.rstd[:, :],
                                                        op0=ALU.mult, op1=ALU.mult))
                    link(nc.vector.tensor_tensor(newton[:, :], newton[:, :], var[:, :], ALU.mult))
                    link(nc.vector.scalar_tensor_tensor(out=t.rstd[:, :], in0=newton[:, :], scalar=1.5, in1=t.rstd[:, :],
                                                        op0=ALU.add, op1=ALU.mult))

            @block.gpsimd
            def _(pool):
                nc.gpsimd.memset(t.ident32[:, :], 0.0).then_inc(zero_set, 1)
                pool.wait_ge(zero_set, 1)
                nc.gpsimd.affine_select(out=t.ident32[:, :], in_=t.ident32[:, :], compare_op=ALU.not_equal, fill=1.0,
                                        base=0, pattern=[[-1, P]], channel_multiplier=1).then_inc(zero_set, 1)
                pool.wait_ge(zero_set, 2)
                nc.gpsimd.tensor_copy(t.ident16[:, :], t.ident32[:, :])
                nc.gpsimd.memset(t.ones[:, :], 1.0)
                pool.wait_ge(key_part, 1)
                nc.gpsimd.partition_all_reduce(whole[:, 0:4], part[:, 0:4], P, ABSMAX).then_inc(whole_max, 1)

                def lo_out(i, value):
                    for o in range(KC):
                        pool.wait_ge(out_hi, KC * i + o + 1)
                        if value:
                            hi = t.v[:, bass.ds((i - NT) * (KC * D) + o * D, D)]
                            lo = t.v[:, bass.ds((i - NT) * (KC * D) + o * D + D * N // P, D)]
                        else:
                            hi = t.w[:, bass.ds(i * TILE + o * N, TILE)]
                            lo = t.w[:, bass.ds(i * TILE + (KC + o) * N, TILE)]
                        nc.gpsimd.tensor_tensor(lo, flat[:, o % 2, :], hi, ALU.subtract).then_inc(out_lo, 1)

                with pool.Fori(0, NT - 1) as i:
                    lo_out(i, False)
                pool.wait_ge(value_part, 1)
                nc.gpsimd.partition_all_reduce(whole[:, 4:5], part[:, 4:5], P, ABSMAX).then_inc(whole_max, 1)
                lo_out(NT - 1, False)
                with pool.Fori(NT, 2 * NT) as i:
                    lo_out(i, True)


def attend(nc, t, x, adj_steps, out):
    with ExitStack() as ctx:
        sb = lambda name, shape, dt: ctx.enter_context(nc.sbuf_tensor(name, shape, dt))
        sem = lambda name: ctx.enter_context(nc.semaphore(name))
        pb = lambda name, shape, dt: ctx.enter_context(nc.psum_tensor(name, shape, dt))

        ring = sb("ring", [P, RING * STEP], F32)
        adj = sb("adj", [P, 2, STEP], F32)
        hT = sb("hT", [P, 2 * 2 * KC * NB], F16)
        mask = sb("mask", [P, STEP], F32)
        ph = sb("ph", [P, 2, 2, STEP], F16)
        col_max = sb("col_max", [P, STEP], F32)
        col_sum = sb("col_sum", [P, STEP], F32)
        x_ln = sb("x_ln", [P, NS, D], F32)
        h16 = sb("h16", [P, NS, 2, D], F16)
        x_out = sb("x_out", [P, NS, D], F32)
        max_n = sb("max_n", [P, NS], F32)
        rsum = sb("rsum", [P, NS], F32)

        scores = [pb(f"scores{b}", [P, STEP], F32) for b in range(2)]
        acc = [pb(f"acc{b}", [P, D], F32) for b in range(NS)]
        turned = [pb(f"turned{b}", [P, KC, NB], F16) for b in range(2)]
        max_bank = pb("max_bank", [P, NB], F32)
        row_bank = pb("row_bank", [P, D], F32)

        adj_in = [sem(f"adj_in{s}") for s in range(2)]
        xln_in, xout_in, xout_biased, stored = sem("xln_in"), sem("xout_in"), sem("xout_biased"), sem("stored")
        centred, h_hi, h_lo, h_turned, h_ready = sem("centred"), sem("h_hi"), sem("h_lo"), sem("h_turned"), sem("h_ready")
        scores_ready = sem("scores_ready")
        scored = sem("scored")
        magnitude = sem("magnitude")
        mask_ready = sem("mask_ready")
        penalised = sem("penalised")
        maxed = sem("maxed")
        max_folded = sem("max_folded")
        max_turned = sem("max_turned")
        max_found = sem("max_found")
        max_spread = sem("max_spread")
        shifted = sem("shifted")
        exped = sem("exped")
        p_hi, p_lo = sem("p_hi"), sem("p_lo")
        summed = sem("summed")
        multiplied = sem("multiplied")
        sums_folded = sem("sums_folded")
        rows_summed = sem("rows_summed")
        sum_inv, sum_scaled = sem("sum_inv"), sem("sum_scaled")
        rows_out = sem("rows_out")

        ring_slot = lambda g: ring[:, bass.ts(g % RING, STEP)]
        halves = lambda a: a.rearrange("p (c n) -> p c n", c=CH)

        with nc.Block() as block:

            @block.sync
            def _(sp):
                def load_adj(j, p, s):
                    g = STEPS * j + p
                    after(sp, scored, g - 1)
                    sp.dma_start(adj[:, s, :], adj_steps[bass.ts(g, P), :]).then_inc(adj_in[s], 16)

                def load_x(buf, j, done):
                    sp.dma_start(buf[:, :, :], x[bass.ts(j, NB), :].rearrange("(s p) d -> p s d", p=P)).then_inc(done, 16)

                def store(j):
                    sp.wait_ge(rows_out, j + 1)
                    sp.dma_start(out[bass.ts(j, NB), :].rearrange("(s p) d -> p s d", p=P), x_out[:, :, :]).then_inc(stored, 16)

                def iteration(j):
                    first, second = isinstance(j, int) and j == 0, isinstance(j, int) and j == 1
                    for p in range(4):
                        load_adj(j, p, p % 2)
                    if not (first or second):
                        store(j - 2)
                    with sp.Fori(2, STEPS // 2) as q:
                        for s in range(2):
                            load_adj(j, 2 * q + s, s)
                    if not first:
                        if not second:
                            sp.wait_ge(stored, 16 * (j - 1))
                        load_x(x_out, j - 1, xout_in)
                    if not (isinstance(j, int) and j + 2 >= BLOCKS):
                        sp.wait_ge(h_lo, NS * (j + 2))
                        load_x(x_ln, j + 2, xln_in)

                load_x(x_ln, 0, xln_in)
                sp.wait_ge(h_lo, NS)
                load_x(x_ln, 1, xln_in)
                iteration(0)
                iteration(1)
                with sp.Fori(2, BLOCKS - 2) as j:
                    iteration(j)
                iteration(BLOCKS - 2)
                iteration(BLOCKS - 1)
                store(BLOCKS - 2)
                sp.wait_ge(stored, 16 * (BLOCKS - 1))
                load_x(x_out, BLOCKS - 1, xout_in)
                store(BLOCKS - 1)
                sp.wait_ge(stored, 16 * BLOCKS)

            @block.tensor
            def _(pe):
                def score(j, p, b):
                    g = STEPS * j + p
                    if isinstance(p, int) and p == 0:
                        pe.wait_ge(h_ready, 2 * (j + 1))
                    after(pe, scored, g - 1)
                    for c in range(CH):
                        for n, (d, (a, e)) in enumerate([(d, ab) for d in range(KC) for ab in PASSES]):
                            w = t.w[:, bass.ds((a * KC + d) * N + c * P + p * (CH * P), P)]
                            h = hT[:, bass.ds((j % 2) * (2 * KC * NB) + (e * KC + d) * NB, NB)]
                            last = nc.tensor.matmul(scores[b][:, c * NB:(c + 1) * NB], w, h,
                                                    start=(n == 0), stop=(n == 3 * KC - 1))
                    last.then_inc(scores_ready, 1)

                def times_v(j, p, b):
                    g = STEPS * j + p
                    first, final = isinstance(p, int) and p == 0, isinstance(p, int) and p == STEPS - 1
                    pe.wait_ge(p_hi, g + 1)
                    pe.wait_ge(p_lo, g + 1)
                    if first:
                        after(pe, rows_out, j)
                    for c in range(CH):
                        for s in range(NS):
                            for n, (a, e) in enumerate(PASSES):
                                pr = ph[:, b, a, c * NB + s * P:c * NB + (s + 1) * P]
                                v = t.v[:, bass.ds(e * (D * N // P) + c * D + p * (CH * D), D)]
                                last = nc.tensor.matmul(acc[s][:, :], pr, v, start=first and c == 0 and n == 0,
                                                        stop=final and c == CH - 1 and n == 2)
                    last.then_inc(multiplied, 1)

                def turn_h(k, s):
                    pe.wait_ge(h_hi, NS * k + s + 1)
                    pe.wait_ge(h_lo, NS * k + s + 1)
                    if s == 0:
                        after(pe, h_ready, 2 * k)
                    for a in range(2):
                        for d in range(KC):
                            last = nc.tensor.transpose(turned[a][:, d, s * P:(s + 1) * P],
                                                       h16[:, s, a, d * P:(d + 1) * P], t.ident16[:, :])
                    last.then_inc(h_turned, 1)

                def turn_max(j):
                    pe.wait_ge(max_folded, j + 1)
                    after(pe, sum_inv, j - 1)
                    for s in range(NS):
                        last = nc.tensor.transpose(row_bank[:, s * P:(s + 1) * P], col_max[:, s * P:(s + 1) * P], t.ident32[:, :])
                    last.then_inc(max_turned, 1)

                def spread_max(j):
                    pe.wait_ge(max_found, j + 1)
                    after(pe, shifted, STEPS * j)
                    for s in range(NS):
                        last = nc.tensor.transpose(max_bank[:, s * P:(s + 1) * P], max_n[:, s:s + 1].to_broadcast([P, P]),
                                                   t.ident32[:, :])
                    last.then_inc(max_spread, 1)

                def sum_rows(j):
                    pe.wait_ge(sums_folded, j + 1)
                    pe.wait_ge(max_found, min(j + 2, BLOCKS) if isinstance(j, int) else j + 2)
                    for s in range(NS):
                        last = nc.tensor.matmul(row_bank[:, s:s + 1], col_sum[:, s * P:(s + 1) * P], t.ones[:, :])
                    last.then_inc(rows_summed, 1)

                def iteration(j):
                    fixed = isinstance(j, int)
                    score(j, 0, 0)
                    if not (fixed and j == 0):
                        spread_max(j - 1)
                    if not (fixed and j < 2):
                        sum_rows(j - 2)
                    score(j, 1, 1)

                    def step(p, b):
                        score(j, p, b)
                        if not (fixed and j == 0):
                            times_v(j - 1, p - 2, b)

                    step(2, 0)
                    step(3, 1)
                    with pe.Fori(2, STEPS // 2 - 1) as q:
                        for s in range(2):
                            step(2 * q + s, s)
                    if not (fixed and j == BLOCKS - 1):
                        turn_h(j + 1, 0)
                        turn_h(j + 1, 1)
                    step(STEPS - 2, 0)
                    step(STEPS - 1, 1)
                    if not (fixed and j == 0):
                        times_v(j - 1, STEPS - 2, 0)
                        times_v(j - 1, STEPS - 1, 1)
                    turn_max(j)

                turn_h(0, 0)
                turn_h(0, 1)
                iteration(0)
                iteration(1)
                with pe.Fori(2, BLOCKS - 1) as j:
                    iteration(j)
                iteration(BLOCKS - 1)
                last_block = BLOCKS - 1
                spread_max(last_block)
                sum_rows(last_block - 1)
                times_v(last_block, 0, 0)
                times_v(last_block, 1, 1)
                with pe.Fori(1, STEPS // 2 - 1) as q:
                    for s in range(2):
                        times_v(last_block, 2 * q + s, s)
                times_v(last_block, STEPS - 2, 0)
                times_v(last_block, STEPS - 1, 1)
                sum_rows(last_block)

            @block.vector
            def _(dve):
                def with_adj(j, p, b):
                    g = STEPS * j + p
                    slot = ring_slot(g)
                    dve.wait_ge(scores_ready, g + 1)
                    dve.wait_ge(adj_in[b], 8 * STEPS * j + 8 * (p - b) + 16)
                    for c in range(CH):
                        last = nc.vector.scalar_tensor_tensor(
                            out=slot[:, c * NB:(c + 1) * NB], in0=scores[b][:, c * NB:(c + 1) * NB],
                            scalar=t.c[:, bass.ds(CH * p + c, 1)], in1=adj[:, b, c * NB:(c + 1) * NB],
                            op0=ALU.add, op1=ALU.mult)
                    last.then_inc(scored, 1)

                def mask_scores(j, p):
                    g = STEPS * j + p
                    slot = ring_slot(g)
                    dve.wait_ge(magnitude, g + 1)
                    nc.vector.tensor_scalar(mask[:, :], mask[:, :], t.threshold[:, 0:1], t.masked[:, 0:1],
                                            ALU.is_lt, ALU.mult).then_inc(mask_ready, 1)
                    dve.wait_ge(mask_ready, g + 1)
                    nc.vector.tensor_tensor(slot, mask[:, :], slot, ALU.add).then_inc(penalised, 1)
                    dve.wait_ge(penalised, g + 1)
                    if isinstance(p, int) and p == 0:
                        after(dve, max_turned, j)
                        nc.vector.tensor_scalar(col_max[:, :], slot, 1.0, None, ALU.mult).then_inc(maxed, 1)
                    else:
                        dve.wait_ge(maxed, g)
                        nc.vector.tensor_tensor(col_max[:, :], col_max[:, :], slot, ALU.max).then_inc(maxed, 1)

                def shift(j, p):
                    g = STEPS * j + p
                    slot = halves(ring_slot(g))
                    if isinstance(p, int) and p == 0:
                        dve.wait_ge(max_spread, j + 1)
                    nc.vector.tensor_tensor(slot, slot, max_bank[:, :].unsqueeze(1).to_broadcast([P, CH, NB]),
                                            ALU.subtract).then_inc(shifted, 1)

                def low_half(j, p, b):
                    g = STEPS * j + p
                    dve.wait_ge(p_hi, g + 1)
                    nc.vector.tensor_tensor(ph[:, b, 1, :], t.p[:, b, :], ph[:, b, 0, :], ALU.subtract).then_inc(p_lo, 1)

                def fold_max(j):
                    dve.wait_ge(maxed, STEPS * (j + 1))
                    nc.vector.tensor_tensor(col_max[:, 0:NB], col_max[:, 0:NB], col_max[:, NB:2 * NB], ALU.max).then_inc(max_folded, 1)

                def find_max(j):
                    dve.wait_ge(max_turned, j + 1)
                    nc.vector.tensor_reduce(max_n[:, :], row_bank[:, 0:NB].rearrange("p (s k) -> p s k", s=NS),
                                            AX.X, ALU.max).then_inc(max_found, 1)

                def rows_to_output(j):
                    dve.wait_ge(rows_summed, j + 1)
                    nc.vector.reciprocal(rsum[:, :], row_bank[:, 0:NS]).then_inc(sum_inv, 1)
                    dve.wait_ge(sum_inv, j + 1)
                    nc.vector.tensor_scalar(rsum[:, :], rsum[:, :], t.inv_sigma_v[:, 0:1], None, ALU.mult).then_inc(sum_scaled, 1)
                    dve.wait_ge(sum_scaled, j + 1)
                    dve.wait_ge(multiplied, STEPS * (j + 1))
                    dve.wait_ge(xout_biased, j + 1)
                    for s in range(NS):
                        last = nc.vector.scalar_tensor_tensor(out=x_out[:, s, :], in0=acc[s][:, :], scalar=rsum[:, s:s + 1],
                                                              in1=x_out[:, s, :], op0=ALU.mult, op1=ALU.add)
                    last.then_inc(rows_out, 1)

                def centre(k, s):
                    if s == 0:
                        dve.wait_ge(xln_in, 16 * (k + 1))
                    nc.vector.tensor_scalar(x_ln[:, s, :], x_ln[:, s, :], t.mean[:, bass.ds(NS * k + s, 1)],
                                            t.rstd[:, bass.ds(NS * k + s, 1)], ALU.subtract, ALU.mult).then_inc(centred, 1)

                def low_h(k, s):
                    dve.wait_ge(h_hi, NS * k + s + 1)
                    nc.vector.scalar_tensor_tensor(out=h16[:, s, 1, :], in0=x_ln[:, s, :], scalar=0.0, in1=h16[:, s, 0, :],
                                                   op0=ALU.max, op1=ALU.subtract).then_inc(h_lo, 1)

                def both(j, p, b):
                    with_adj(j, p, b)
                    shift(j - 1, p)
                    mask_scores(j, p)
                    if isinstance(p, int) and p == STEPS - 1:
                        fold_max(j)
                    low_half(j - 1, p, b)

                def iteration(j):
                    fixed = isinstance(j, int)
                    before = not (fixed and j == 0)
                    more = not (fixed and j == BLOCKS - 1)
                    if before:
                        find_max(j - 1)
                        with_adj(j, 0, 0)
                        shift(j - 1, 0)
                        if not (fixed and j < 2):
                            rows_to_output(j - 2)
                        with_adj(j, 1, 1)
                        shift(j - 1, 1)
                        low_half(j - 1, 0, 0)
                        mask_scores(j, 0)
                        low_half(j - 1, 1, 1)
                        mask_scores(j, 1)
                    else:
                        for p in range(2):
                            with_adj(j, p, p)
                            mask_scores(j, p)

                    def step(p, b):
                        if before:
                            both(j, p, b)
                        else:
                            with_adj(j, p, b)
                            mask_scores(j, p)

                    def pairs(lo, hi):
                        with dve.Fori(lo, hi) as q:
                            step(2 * q, 0)
                            step(2 * q + 1, 1)

                    pairs(1, 3)
                    if more:
                        centre(j + 1, 0)
                    step(6, 0)
                    if more:
                        low_h(j + 1, 0)
                    step(7, 1)
                    if more:
                        centre(j + 1, 1)
                    step(8, 0)
                    if more:
                        low_h(j + 1, 1)
                    step(9, 1)
                    pairs(5, STEPS // 2 - 1)
                    step(STEPS - 2, 0)
                    step(STEPS - 1, 1)
                    if not before:
                        fold_max(j)

                for s in range(NS):
                    centre(0, s)
                    low_h(0, s)
                iteration(0)
                iteration(1)
                with dve.Fori(2, BLOCKS - 1) as j:
                    iteration(j)
                iteration(BLOCKS - 1)
                find_max(BLOCKS - 1)
                rows_to_output(BLOCKS - 2)
                for p in range(2):
                    shift(BLOCKS - 1, p)
                with dve.Fori(1, STEPS // 2) as q:
                    for s in range(2):
                        shift(BLOCKS - 1, 2 * q + s)
                        low_half(BLOCKS - 1, 2 * q - 2 + s, s)
                for s in range(2):
                    low_half(BLOCKS - 1, STEPS - 2 + s, s)
                rows_to_output(BLOCKS - 1)

            @block.scalar
            def _(act):
                def exps(j, p, b):
                    g = STEPS * j + p
                    act.wait_ge(shifted, g + 1)
                    after(act, p_lo, g - 1)
                    after(act, summed, g - 1)
                    nc.scalar.activation(t.p[:, b, :], ring_slot(g), ACT.Exp, bias=t.log_top[:, 0:1],
                                         scale=t.inv_kappa[:, 0:1]).then_inc(exped, 1)
                    act.wait_ge(exped, g + 1)
                    after(act, multiplied, g - 1)
                    nc.scalar.activation(ph[:, b, 0, :], t.p[:, b, :], ACT.Copy).then_inc(p_hi, 1)

                def magnitudes(j, p):
                    g = STEPS * j + p
                    act.wait_ge(scored, g + 1)
                    after(act, mask_ready, g)
                    after(act, penalised, g)
                    nc.scalar.activation(mask[:, :], ring_slot(g), ACT.Abs).then_inc(magnitude, 1)

                def high_h(k, s):
                    n = NS * k + s + 1
                    act.wait_ge(centred, n)
                    after(act, h_turned, n - NS)
                    nc.scalar.activation(h16[:, s, 0, :], x_ln[:, s, :], ACT.Relu).then_inc(h_hi, 1)

                def take_h(k):
                    act.wait_ge(h_turned, NS * (k + 1))
                    after(act, scores_ready, STEPS * (k - 1))
                    for a in range(2):
                        nc.scalar.activation(hT[:, bass.ds((k % 2) * (2 * KC * NB) + a * (KC * NB), KC * NB)],
                                             turned[a][:, :, :].rearrange("p c n -> p (c n)"), ACT.Copy).then_inc(h_ready, 1)

                def iteration(j):
                    fixed = isinstance(j, int)
                    before = not (fixed and j == 0)
                    more = not (fixed and j == BLOCKS - 1)

                    def step(p, b):
                        if not before:
                            magnitudes(j, p)
                        elif isinstance(p, int) and p < 2:
                            exps(j - 1, p, b)
                            magnitudes(j, p)
                        else:
                            magnitudes(j, p)
                            exps(j - 1, p, b)

                    def pairs(lo, hi):
                        with act.Fori(lo, hi) as q:
                            step(2 * q, 0)
                            step(2 * q + 1, 1)

                    for p in range(2):
                        step(p, p)
                    pairs(1, 3)
                    if more:
                        high_h(j + 1, 0)
                    step(6, 0)
                    step(7, 1)
                    if more:
                        high_h(j + 1, 1)
                    pairs(4, STEPS // 2 - 1)
                    if more:
                        take_h(j + 1)
                    step(STEPS - 2, 0)
                    step(STEPS - 1, 1)

                high_h(0, 0)
                high_h(0, 1)
                take_h(0)
                iteration(0)
                iteration(1)
                with act.Fori(2, BLOCKS - 1) as j:
                    iteration(j)
                iteration(BLOCKS - 1)
                with act.Fori(0, STEPS // 2) as q:
                    for s in range(2):
                        exps(BLOCKS - 1, 2 * q + s, s)

            @block.gpsimd
            def _(pool):
                def add_up(j, p, b):
                    g = STEPS * j + p
                    pool.wait_ge(exped, g + 1)
                    if isinstance(p, int) and p == 1:
                        after(pool, rows_summed, j)
                        nc.gpsimd.tensor_tensor(col_sum[:, :], t.p[:, 0, :], t.p[:, 1, :], ALU.add).then_inc(summed, 2)
                    else:
                        pool.wait_ge(summed, g)
                        nc.gpsimd.tensor_tensor(col_sum[:, :], col_sum[:, :], t.p[:, b, :], ALU.add).then_inc(summed, 1)

                def block_sums(j):
                    add_up(j, 1, 1)
                    with pool.Fori(1, STEPS // 2) as q:
                        for s in range(2):
                            add_up(j, 2 * q + s, s)
                    pool.wait_ge(summed, STEPS * (j + 1))
                    nc.gpsimd.tensor_tensor(col_sum[:, 0:NB], col_sum[:, 0:NB], col_sum[:, NB:2 * NB], ALU.add).then_inc(sums_folded, 1)
                    pool.wait_ge(xout_in, 16 * (j + 1))
                    for s in range(NS):
                        last = nc.gpsimd.tensor_tensor(x_out[:, s, :], x_out[:, s, :], t.out_bias[:, :], ALU.add)
                    last.then_inc(xout_biased, 1)

                block_sums(0)
                with pool.Fori(1, BLOCKS) as j:
                    block_sums(j)


class Kept:
    pass


def build(nc, x, adj_steps, kv_rows, kv_cols, wq, wk, wv, wmT, bq, bk, bv, bm, out):
    with ExitStack() as ctx:
        sb = lambda name, shape, dt: ctx.enter_context(nc.sbuf_tensor(name, shape, dt))
        t = Kept()
        t.w = sb("w", [P, 2 * KC * N], F16)
        t.v = sb("v", [P, 2 * (N // P) * D], F16)
        t.p = sb("p", [P, 2, STEP], F32)
        t.out_bias = sb("out_bias", [P, D], F32)
        t.ident32 = sb("ident32", [P, P], F32)
        t.ident16 = sb("ident16", [P, P], F16)
        t.ones = sb("ones", [P, 1], F32)
        t.c = sb("c", [P, N // P], F32)
        t.mean = sb("mean", [P, N // P], F32)
        t.rstd = sb("rstd", [P, N // P], F32)
        column = lambda name: sb(name, [P, 1], F32)
        t.inv_kappa, t.threshold, t.masked = column("inv_kappa"), column("threshold"), column("masked")
        t.log_top, t.inv_sigma_v = column("log_top"), column("inv_sigma_v")
        fold_and_project(nc, t, x, kv_rows, kv_cols, wq, wk, wv, wmT, bq, bk, bv, bm)
        attend(nc, t, x, adj_steps, out)


def kernel(x, adj, L0_gnn_key, L0_gnn_value, L0_gnn_Wq, L0_gnn_bq, L0_gnn_Wk, L0_gnn_bk, L0_gnn_Wv, L0_gnn_bv,
           L0_gnn_Wm, L0_gnn_bm):
    import numpy as np
    import concourse.bacc as bacc
    from concourse import mybir as mb
    from concourse.bass_utils import run_bass_kernel_spmd

    adj = np.asarray(adj)
    kv = np.concatenate([np.asarray(L0_gnn_key), np.asarray(L0_gnn_value)], axis=0)
    steps = adj.reshape(BLOCKS, NB, STEPS, CH, P).transpose(0, 2, 4, 3, 1).reshape(BLOCKS * STEPS * P, STEP)
    arrays = {
        "x": x, "adj_steps": steps, "kv_rows": kv, "kv_cols": kv.T, "wq": L0_gnn_Wq, "wk": L0_gnn_Wk,
        "wv": L0_gnn_Wv, "wmT": np.asarray(L0_gnn_Wm).T, "bq": L0_gnn_bq, "bk": L0_gnn_bk, "bv": L0_gnn_bv, "bm": L0_gnn_bm,
    }
    arrays = {k: np.ascontiguousarray(a) for k, a in arrays.items()}
    nc = bacc.Bacc("TRN2", target_bir_lowering=False, num_devices=1)
    args = [nc.dram_tensor(k, a.shape, mb.dt.from_np(a.dtype), kind="ExternalInput").ap() for k, a in arrays.items()]
    args.append(nc.dram_tensor("out", (N, D), mb.dt.from_np(np.dtype("float32")), kind="ExternalOutput").ap())
    build(nc, *args)
    r = run_bass_kernel_spmd(nc, [arrays], core_ids=[0])
    return r.results[0]["out"]
```

```python
from contextlib import ExitStack

import concourse.bass as bass
from concourse import mybir

ALU = mybir.AluOpType
ACT = mybir.ActivationFunctionType
F32 = mybir.dt.float32
F16 = mybir.dt.float16
BF16 = mybir.dt.bfloat16
U32 = mybir.dt.uint32
AX = mybir.AxisListType
ABSMAX = bass.bass_isa.ReduceOp.absmax

P = 128
N = 4096
D = 512
KC = D // P
TILE = 512
NT = N // TILE
NB = 256
BLOCKS = N // NB
NS = NB // P
HP = 2
XR = N // P
CH = 2
STEPS = N // (CH * P)
STEP = CH * NB
RING = STEPS + 2
TOP = 2.0 ** 14
FLOOR = 2.0 ** -60
H_SCALE = 512.0
THRESHOLD = 1e-5
MASKED = -1e9
EPS = 1e-5
NEWTON = 3
LOG_TOP = 8.25
SCORE_DIV = float(N) ** 0.5
PASSES = ((0, 0), (0, 1), (1, 0))


def after(eng, sem, value):
    if not (isinstance(value, int) and value <= 0):
        eng.wait_ge(sem, value)


def fold_and_project(nc, t, x, x_cols, row_stats, kv_rows, kv_cols, wq, wk, wv, wmT, bq, bk, bv, bm):
    with ExitStack() as ctx:
        sb = lambda name, shape, dt: ctx.enter_context(nc.sbuf_tensor(name, shape, dt))
        sem = lambda name: ctx.enter_context(nc.semaphore(name))

        def borrow(i, n):
            return t.v[:, i * 4096:(i + n) * 4096].bitcast(F32)
        wk_s, wq_s, wv_s, wm_s = (borrow(i, 1).rearrange("p (o d) -> p o d", o=KC) for i in range(4))
        g32, m32 = borrow(4, 1), borrow(5, 1)
        rows = [borrow(6 + s, 1) for s in range(2)]

        cols32 = sb("cols32", [P, 2, KC * TILE], F32)
        cols = sb("cols", [P, 2, 2, KC * TILE], F16)
        gh = sb("gh", [P, 2, KC * D], F16)
        mh = sb("mh", [P, 2, KC * D], F16)
        flat = sb("flat", [P, 2, TILE], F32)
        u_bc = sb("u_bc", [P, D], F32)
        x_rows = t.hT[:, :].bitcast(F32).rearrange("p (s d) -> p s d", s=2)
        stats = sb("stats", [P, XR, 6], F32)
        mean_rstd = sb("mean_rstd", [P, 2, XR], F32)
        mean, rstd = mean_rstd[:, 0, :], mean_rstd[:, 1, :]
        vecs = sb("vecs", [P, 3, KC], F32)
        wb = sb("wb", [P, KC], F32)
        wb_scaled = sb("wb_scaled", [P, KC], F32)
        craw = sb("craw", [P, N // P], F32)
        bqbk = sb("bqbk", [P, 1], F32)
        tile_sum = sb("tile_sum", [P, 2 * NT], F32)
        var = sb("var", [P, XR], F32)
        newton = sb("newton", [P, XR], F32)
        part = sb("part", [P, 5], F32)
        whole = sb("whole", [P, 5], F32)
        pw = sb("pw", [P, 8], F32)
        sc = sb("sc", [P, 16], F32)
        scratch = t.hT[:, :].bitcast(F32)
        ps = t.banks

        wq_in, wv_in, wm_in, bq_in, vecs_in, bm_in = (sem(s + "_in") for s in ("wq", "wv", "wm", "bq", "vecs", "bm"))
        wk_in = [sem(f"wk_in{i}") for i in range(2)]
        rows_in = [sem(f"rows_in{s}") for s in range(2)]
        cols_in = [sem(f"cols_in{s}") for s in range(2)]
        x_in = [sem(f"x_in{s}") for s in range(2)]
        x_free = sem("x_free")
        dotted = sem("dotted")
        measured = sem("measured")
        stats_ready = sem("stats_ready")
        stats_written = sem("stats_written")
        bias_folded = sem("bias_folded")
        folded = sem("folded")
        taken = sem("taken")
        zero_set = sem("zero_set")
        dve_seq = sem("dve_seq")
        part_ready = sem("part_ready")
        whole_max = sem("whole_max")
        scales = sem("scales")
        weight_hi = sem("weight_hi")
        weight_lo = sem("weight_lo")
        cols_hi = sem("cols_hi")
        cols_lo = sem("cols_lo")
        bank_ready = sem("bank_ready")
        flat_ready = sem("flat_ready")
        out_hi = sem("out_hi")
        flat_free = sem("flat_free")

        rows_slots = [(rows[s], rows_in[s]) for s in range(2)]
        cols_slots = [(cols32[:, s, :], cols_in[s]) for s in range(2)]
        key_slots = rows_slots + cols_slots + cols_slots + rows_slots

        OF_G, OF_B, OF_K, OF_M, OF_V = range(5)
        SK, SG, SV, SM, ALPHA_W, ALPHA_V, SIG_W, CSCALE, T0, T1, T2 = range(11)
        col = lambda a, i: a[:, i:i + 1]

        with nc.Block() as block:

            @block.sync
            def _(sp):
                sp.dma_start(vecs[:, 0, :], bq.rearrange("(c p) -> p c", p=P), allow_slow_non_contiguous=True).then_inc(bq_in, 16)
                for i in range(2):
                    sp.dma_start(wk_s[:, 2 * i:2 * i + 2, :],
                                 wk[bass.ts(i, D // 2), :].rearrange("(o p) d -> p o d", p=P)).then_inc(wk_in[i], 16)
                sp.dma_start(wq_s, wq.rearrange("(o p) d -> p o d", p=P)).then_inc(wq_in, 16)
                sp.dma_start(vecs[:, 1, :], bk.rearrange("(c p) -> p c", p=P), allow_slow_non_contiguous=True).then_inc(vecs_in, 16)
                sp.dma_start(vecs[:, 2, :], bv.rearrange("(c p) -> p c", p=P), allow_slow_non_contiguous=True).then_inc(vecs_in, 16)

                def load_rows(i, buf, done):
                    sp.dma_start(buf.rearrange("p (r d) -> p r d", r=KC),
                                 kv_rows[bass.ts(i, TILE), :].rearrange("(r p) d -> p r d", p=P)).then_inc(done, 16)

                def load_cols(i, s):
                    sp.dma_start(cols32[:, s, :].rearrange("p (e m) -> p e m", e=KC),
                                 kv_cols[:, bass.ts(i, TILE)].rearrange("(e p) m -> p e m", p=P)).then_inc(cols_in[s], 16)

                def load_values(i, s):
                    sp.wait_ge(measured, NT + i - 1)
                    load_rows(NT + i, rows[s], rows_in[s])

                def key_used(n):
                    sp.wait_ge(dotted, KC * n)
                    sp.wait_ge(measured, n)

                def load_x(k, s):
                    sp.wait_ge(x_free, k + 1)
                    sp.dma_start(x_rows[:, s, :].rearrange("p (r d) -> p r d", r=NS),
                                 x.rearrange("(p r) d -> p r d", p=P)[:, bass.ds(NS * k, NS), :]).then_inc(x_in[s], 16)

                for i in range(4):
                    load_rows(i, *key_slots[i])
                sp.dma_start(wv_s, wv.rearrange("(o p) d -> p o d", p=P)).then_inc(wv_in, 16)
                sp.dma_start(wm_s, wmT.rearrange("(o p) d -> p o d", p=P)).then_inc(wm_in, 16)
                sp.dma_start(t.out_bias[:, :], bm.partition_broadcast(P)).then_inc(bm_in, 16)
                for i in range(4, NT):
                    key_used(i - 1 if i < 6 else i - 5)
                    load_rows(i, *key_slots[i])
                for s in range(2):
                    key_used(5 + s)
                    load_cols(s, s)
                for s in range(2):
                    key_used(7 + s)
                    load_rows(NT + s, rows[s], rows_in[s])
                load_values(2, 0)
                load_values(3, 1)

                def load_step(i, s, values, stats):
                    sp.wait_ge(cols_lo, i - 1)
                    load_cols(i, s)
                    if values:
                        load_values(i + 2, s)
                    if stats:
                        load_x(2 * i - 4, 0)
                        load_x(2 * i - 3, 1)

                with sp.Fori(1, 3) as i2:
                    for s in range(2):
                        load_step(2 * i2 + s, s, True, True)
                with sp.Fori(3, NT // 2 + 1) as i2:
                    for s in range(2):
                        load_step(2 * i2 + s, s, False, True)
                for s in range(2):
                    load_step(NT + 2 + s, s, False, False)
                load_step(NT + 4, 0, False, False)
                sp.wait_ge(stats_ready, 1)
                sp.dma_start(row_stats.rearrange("a (p r) -> p a r", p=P), mean_rstd[:, :, :]).then_inc(stats_written, 16)
                sp.wait_ge(stats_written, 16)
                load_h_inputs(sp, t, x_cols, row_stats, 0)
                load_step(NT + 5, 1, False, False)
                with sp.Fori(NT // 2 + 3, NT) as i2:
                    for s in range(2):
                        load_step(2 * i2 + s, s, False, False)

            @block.tensor
            def _(pe):
                def product(bank, w, x):
                    for o in range(KC):
                        last = nc.tensor.matmul(bank, w(o), x(o), start=(o == 0), stop=(o == KC - 1))
                    last.then_inc(folded, 1)

                row = lambda i: (lambda o: vecs[:, i, o:o + 1].to_broadcast([P, P]))
                chunk = lambda a, e: (lambda o: a[:, o, e * P:(e + 1) * P])
                full = lambda a: (lambda o: a[:, o, :])
                colv = lambda i: (lambda o: vecs[:, i, o:o + 1])

                pe.wait_ge(bq_in, 16)
                for o in range(KC):
                    if o % 2 == 0:
                        pe.wait_ge(wk_in[o // 2], 16)
                    last = nc.tensor.matmul(ps[4][:, :], row(0)(o), full(wk_s)(o), start=(o == 0), stop=(o == KC - 1))
                last.then_inc(folded, 1)
                pe.wait_ge(wq_in, 16)
                for e in range(KC):
                    product(ps[e][:, :], chunk(wk_s, e), full(wq_s))
                pe.wait_ge(vecs_in, 32)
                for d in range(KC):
                    product(ps[5][:, d:d + 1], chunk(wq_s, d), colv(1))
                product(ps[6][:, 0:1], row(0), colv(1))
                pe.wait_ge(wv_in, 16)
                pe.wait_ge(wm_in, 16)
                pe.wait_ge(taken, 5)
                for e in range(KC):
                    product(ps[e][:, :], chunk(wv_s, e), full(wm_s))
                product(ps[7][:, :], row(2), full(wm_s))

                def project(i, s, weights_stay):
                    pe.wait_ge(cols_hi, i + 1)
                    pe.wait_ge(cols_lo, i + 1)
                    for o in range(KC):
                        after(pe, flat_ready, KC * i + o - 7)
                        for n, (e, (a, b)) in enumerate([(e, ab) for e in range(KC) for ab in PASSES]):
                            if weights_stay:
                                l, r = gh[:, a, e * D + o * P:][:, 0:P], cols[:, s, b, e * TILE:(e + 1) * TILE]
                            else:
                                l, r = cols[:, s, a, e * TILE + o * P:][:, 0:P], mh[:, b, e * D:(e + 1) * D]
                            last = nc.tensor.matmul(ps[4 * s + o][:, :], l, r, start=(n == 0), stop=(n == 3 * KC - 1))
                        last.then_inc(bank_ready, 1)

                pe.wait_ge(taken, 11)
                pe.wait_ge(weight_hi, 1)
                pe.wait_ge(weight_lo, 1)
                project(0, 0, True)
                pe.wait_ge(bias_folded, 1)
                project(1, 1, True)
                with pe.Fori(1, NT // 2) as i2:
                    for s in range(2):
                        project(2 * i2 + s, s, True)
                pe.wait_ge(weight_hi, 2)
                pe.wait_ge(weight_lo, 2)
                with pe.Fori(NT // 2, NT) as i2:
                    for s in range(2):
                        project(2 * i2 + s, s, False)

            @block.scalar
            def _(act):
                def take(n, out, bank):
                    act.wait_ge(folded, n)
                    nc.scalar.activation(out, bank, ACT.Copy).then_inc(taken, 1)

                def measure(buf, n):
                    nc.scalar.activation(scratch if isinstance(n, int) and n < NT else buf, buf, ACT.Abs,
                                         accum_out=tile_sum[:, bass.ds(n, 1)]).then_inc(measured, 1)

                def measure_keys(i):
                    buf, loaded = key_slots[i]
                    act.wait_ge(loaded, 16 * (i // 4 + 1))
                    after(act, measured, i)
                    measure(buf, i)

                def measure_values(i, s):
                    act.wait_ge(rows_in[s], 16 * (i // 2 + 3) if isinstance(i, int) else 16 * (i >> 1) + 48)
                    measure(rows[s], NT + i)

                take(1, u_bc[:, :], ps[4][:, :])
                for e in range(KC):
                    measure_keys(e)
                    take(2 + e, g32[:, e * D:(e + 1) * D], ps[e][:, :])
                take(9, wb[:, :], ps[5][:, 0:KC])
                take(10, bqbk[:, :], ps[6][:, 0:1])
                measure_keys(4)
                measure_keys(5)
                act.wait_ge(scales, 1)
                nc.scalar.activation(gh[:, 0, :], g32, ACT.Copy, scale=col(sc, SG)).then_inc(weight_hi, 1)
                measure_keys(6)
                measure_keys(7)
                for e in range(KC - 1):
                    take(11 + e, m32[:, e * D:(e + 1) * D], ps[e][:, :])

                def split(i, s, scale):
                    act.wait_ge(cols_in[s], 16 * (i // 2 + 3) if isinstance(i, int) else 16 * (i >> 1) + 48)
                    if not (isinstance(i, int) and i < 2):
                        act.wait_ge(bank_ready, KC * (i - 1))
                    nc.scalar.activation(cols[:, s, 0, :], cols32[:, s, :], ACT.Copy, scale=col(sc, scale)).then_inc(cols_hi, 1)

                def hi_out(i, banks, value):
                    for o in banks:
                        act.wait_ge(flat_ready, KC * i + o + 1)
                        if value:
                            out = t.v[:, bass.ds((i - NT) * (KC * D) + o * D, D)]
                        else:
                            out = t.w[:, bass.ds(i * TILE + o * N, TILE)]
                        nc.scalar.activation(out, flat[:, o % 2, :], ACT.Copy).then_inc(out_hi, 1)

                def tile_step(i, s, scale, value):
                    hi_out(i - 2, (0, 1), value)
                    split(i, s, scale)
                    hi_out(i - 2, (2, 3), value)

                act.wait_ge(scales, 2)
                split(0, 0, SK)
                take(14, m32[:, 3 * D:4 * D], ps[3][:, :])
                split(1, 1, SK)
                for i in range(4):
                    measure_values(i, i % 2)
                with act.Fori(1, 3) as i2:
                    for s in range(2):
                        tile_step(2 * i2 + s, s, SK, False)
                        measure_values(2 * i2 + s + 2, s)
                tile_step(NT - 2, 0, SK, False)
                act.wait_ge(scales, 3)
                nc.scalar.activation(mh[:, 0, :], m32, ACT.Copy, scale=col(sc, SM)).then_inc(weight_hi, 1)
                tile_step(NT - 1, 1, SK, False)
                tile_step(NT, 0, SV, False)
                tile_step(NT + 1, 1, SV, False)
                act.wait_ge(weight_lo, 2)
                tile_step(NT + 2, 0, SV, True)
                tile_step(NT + 3, 1, SV, True)
                with act.Fori(NT // 2 + 2, NT) as i2:
                    for s in range(2):
                        tile_step(2 * i2 + s, s, SV, True)
                hi_out(2 * NT - 2, range(KC), True)
                for s in range(HP):
                    high_h(act, nc, t, 0, s)
                hi_out(2 * NT - 1, range(KC), True)

            @block.vector
            def _(dve):
                seq = [0]

                def link(ins):
                    seq[0] += 1
                    ins.then_inc(dve_seq, 1)
                    dve.wait_ge(dve_seq, seq[0])

                def dot_keys(i):
                    buf, loaded = key_slots[i]
                    dve.wait_ge(loaded, 16 * (i // 4 + 1))
                    for r in range(KC):
                        after(dve, dotted, KC * i + r - 1)
                        nc.vector.scalar_tensor_tensor(
                            out=t.p[:, r % 2, :], in0=buf[:, r * D:(r + 1) * D], scalar=1.0, in1=u_bc[:, :],
                            op0=ALU.mult, op1=ALU.mult, accum_out=craw[:, KC * i + r:KC * i + r + 1]).then_inc(dotted, 1)

                def power(out, x):
                    link(nc.vector.tensor_scalar(col(pw, T_PW), x, FLOOR, None, ALU.max))
                    link(nc.vector.tensor_scalar(out.bitcast(U32), col(pw, T_PW).bitcast(U32), 0x7F800000, None, ALU.bitwise_and))

                def inverse_scale(out, power_of):
                    link(nc.vector.tensor_scalar(out, power_of, 1.0 / TOP, None, ALU.mult))

                T_PW = 7
                PK, PG, PV_, PM, PW_, = 0, 1, 2, 3, 4

                def weight_lo_of(out, x, scale, hi, n):
                    dve.wait_ge(weight_hi, n)
                    nc.vector.scalar_tensor_tensor(out=out, in0=x, scalar=col(sc, scale), in1=hi,
                                                   op0=ALU.mult, op1=ALU.subtract).then_inc(weight_lo, 1)

                def split_lo(i, s, scale):
                    dve.wait_ge(cols_hi, i + 1)
                    nc.vector.scalar_tensor_tensor(out=cols[:, s, 1, :], in0=cols32[:, s, :], scalar=col(sc, scale),
                                                   in1=cols[:, s, 0, :], op0=ALU.mult, op1=ALU.subtract).then_inc(cols_lo, 1)

                def take_out(i, s, value):
                    for o in range(KC):
                        dve.wait_ge(bank_ready, KC * i + o + 1)
                        dve.wait_ge(flat_free, KC * i + o + 1)
                        if value:
                            ins = nc.vector.tensor_scalar(flat[:, o % 2, :], ps[4 * s + o][:, :], col(sc, ALPHA_V), None, ALU.mult)
                        else:
                            ins = nc.vector.tensor_scalar(flat[:, o % 2, :], ps[4 * s + o][:, :], col(sc, ALPHA_W),
                                                          wb_scaled[:, o:o + 1], ALU.mult, ALU.add)
                        ins.then_inc(flat_ready, 1)

                def x_stats(k, s):
                    dve.wait_ge(x_in[s], 16 * (k // 2 + 1) if isinstance(k, int) else 16 * (k >> 1) + 16)
                    for r in range(NS):
                        last = nc.vector.bn_stats(stats[:, bass.ds(NS * k + r, 1), :].rearrange("p o k -> p (o k)"),
                                                  x_rows[:, s, r * D:(r + 1) * D])
                    last.then_inc(x_free, 1)

                def tile_step(i, s, scale, value, stats):
                    take_out(i - 2, s, value)
                    split_lo(i, s, scale)
                    if stats:
                        x_stats(2 * i - 4, 0)
                        x_stats(2 * i - 3, 1)

                dve.wait_ge(taken, 1)
                for i in range(4):
                    dot_keys(i)

                dve.wait_ge(taken, 6)
                link(nc.vector.tensor_reduce(col(part, OF_G), g32, AX.X, ALU.max, apply_absolute_value=True))
                nc.vector.tensor_reduce(col(part, OF_B), wb[:, :], AX.X, ALU.max, apply_absolute_value=True).then_inc(part_ready, 1)
                dot_keys(4)
                dve.wait_ge(whole_max, 1)
                power(col(pw, PG), col(whole, OF_G))
                inverse_scale(col(sc, T1), col(pw, PG))
                nc.vector.reciprocal(col(sc, SG), col(sc, T1)).then_inc(scales, 1)
                dot_keys(5)
                dve.wait_ge(scales, 1)
                weight_lo_of(gh[:, 1, :], g32, SG, gh[:, 0, :], 1)
                dot_keys(6)
                dve.wait_ge(measured, NT)
                nc.vector.tensor_reduce(col(part, OF_K), tile_sum[:, 0:NT], AX.X, ALU.max).then_inc(part_ready, 1)
                nc.vector.memset(t.log_top[:, :], LOG_TOP).then_inc(x_free, 2)
                dve.wait_ge(whole_max, 2)
                power(col(pw, PK), col(whole, OF_K))
                inverse_scale(col(sc, T0), col(pw, PK))
                nc.vector.reciprocal(col(sc, SK), col(sc, T0)).then_inc(scales, 1)
                dot_keys(7)
                dve.wait_ge(scales, 2)

                split_lo(0, 0, SK)

                link(nc.vector.tensor_scalar(col(sc, T2), col(whole, OF_K), col(pw, PG), 2.0, ALU.mult, ALU.mult))
                link(nc.vector.tensor_tensor(col(sc, T2), col(sc, T2), col(whole, OF_B), ALU.add))
                power(col(pw, PW_), col(sc, T2))
                inverse_scale(col(sc, T2), col(pw, PW_))
                link(nc.vector.reciprocal(col(sc, SIG_W), col(sc, T2)))
                link(nc.vector.tensor_tensor(col(sc, ALPHA_W), col(sc, T0), col(sc, T1), ALU.mult))
                link(nc.vector.tensor_tensor(col(sc, ALPHA_W), col(sc, ALPHA_W), col(sc, SIG_W), ALU.mult))
                link(nc.vector.tensor_scalar(wb_scaled[:, :], wb[:, :], col(sc, SIG_W), None, ALU.mult))
                link(nc.vector.tensor_scalar(col(sc, CSCALE), col(sc, SIG_W), H_SCALE, None, ALU.mult))
                dve.wait_ge(dotted, KC * NT)
                link(nc.vector.tensor_scalar(t.c[:, :], craw[:, :], col(bqbk, 0), col(sc, CSCALE), ALU.add, ALU.mult))
                nc.vector.tensor_scalar(t.inv_kappa[:, :], col(sc, T2), 1.0 / (H_SCALE * SCORE_DIV), None, ALU.mult)
                nc.vector.tensor_scalar(t.threshold[:, :], col(sc, SIG_W), H_SCALE * SCORE_DIV, THRESHOLD, ALU.mult, ALU.mult)
                link(nc.vector.tensor_scalar(t.masked[:, :], col(sc, SIG_W), H_SCALE * SCORE_DIV, MASKED, ALU.mult, ALU.mult))
                dve.wait_ge(bm_in, 16)
                dve.wait_ge(folded, 15)
                nc.vector.tensor_tensor(t.out_bias[:, :], t.out_bias[:, :], ps[7][:, :], ALU.add).then_inc(bias_folded, 1)
                split_lo(1, 1, SK)
                dve.wait_ge(taken, 11)
                link(nc.vector.tensor_reduce(col(part, OF_M), m32, AX.X, ALU.max, apply_absolute_value=True))

                with dve.Fori(1, 3) as i2:
                    for s in range(2):
                        tile_step(2 * i2 + s, s, SK, False, True)
                tile_step(NT - 2, 0, SK, False, True)

                dve.wait_ge(measured, 2 * NT)
                nc.vector.tensor_reduce(col(part, OF_V), tile_sum[:, NT:2 * NT], AX.X, ALU.max).then_inc(part_ready, 1)
                dve.wait_ge(whole_max, 3)
                power(col(pw, PV_), col(whole, OF_V))
                power(col(pw, PM), col(whole, OF_M))
                inverse_scale(col(sc, T0), col(pw, PV_))
                inverse_scale(col(sc, T1), col(pw, PM))
                link(nc.vector.reciprocal(col(sc, SV), col(sc, T0)))
                link(nc.vector.reciprocal(col(sc, SM), col(sc, T1)))
                link(nc.vector.tensor_scalar(col(sc, T2), col(whole, OF_V), col(pw, PM), 2.0, ALU.mult, ALU.mult))
                power(col(pw, PW_), col(sc, T2))
                inverse_scale(t.inv_sigma_v[:, :], col(pw, PW_))
                link(nc.vector.reciprocal(col(sc, T2), t.inv_sigma_v[:, :]))
                link(nc.vector.tensor_tensor(col(sc, ALPHA_V), col(sc, T0), col(sc, T1), ALU.mult))
                nc.vector.tensor_tensor(col(sc, ALPHA_V), col(sc, ALPHA_V), col(sc, T2), ALU.mult).then_inc(scales, 1)
                tile_step(NT - 1, 1, SK, False, True)
                dve.wait_ge(scales, 3)
                weight_lo_of(mh[:, 1, :], m32, SM, mh[:, 0, :], 2)
                tile_step(NT, 0, SV, False, True)
                tile_step(NT + 1, 1, SV, False, True)

                tile_step(NT + 2, 0, SV, True, False)

                dve.wait_ge(x_free, BLOCKS + 2)
                link(nc.vector.tensor_tensor(mean, stats[:, :, 1], stats[:, :, 4], ALU.add))
                link(nc.vector.tensor_tensor(newton[:, :], stats[:, :, 1], stats[:, :, 4], ALU.subtract))
                link(nc.vector.tensor_tensor(var[:, :], stats[:, :, 2], stats[:, :, 5], ALU.add))
                link(nc.vector.tensor_scalar(mean, mean, 0.5, None, ALU.mult))
                link(nc.vector.scalar_tensor_tensor(out=newton[:, :], in0=newton[:, :], scalar=0.25, in1=newton[:, :],
                                                    op0=ALU.mult, op1=ALU.mult))
                link(nc.vector.scalar_tensor_tensor(out=var[:, :], in0=var[:, :], scalar=1.0 / D, in1=newton[:, :],
                                                    op0=ALU.mult, op1=ALU.add))
                link(nc.vector.tensor_scalar(var[:, :], var[:, :], EPS, H_SCALE ** -2, ALU.add, ALU.mult))
                link(nc.vector.tensor_scalar(rstd.bitcast(U32), var[:, :].bitcast(U32), 1, None, ALU.logical_shift_right))
                link(nc.vector.tensor_scalar(rstd.bitcast(U32), rstd.bitcast(U32), -1.0, float(0x5F3759DF),
                                             ALU.mult, ALU.add))
                for i in range(NEWTON):
                    link(nc.vector.scalar_tensor_tensor(out=newton[:, :], in0=rstd, scalar=-0.5, in1=rstd,
                                                        op0=ALU.mult, op1=ALU.mult))
                    link(nc.vector.tensor_tensor(newton[:, :], newton[:, :], var[:, :], ALU.mult))
                    better = nc.vector.scalar_tensor_tensor(out=rstd, in0=newton[:, :], scalar=1.5, in1=rstd,
                                                            op0=ALU.add, op1=ALU.mult)
                    if i < NEWTON - 1:
                        link(better)
                    else:
                        better.then_inc(stats_ready, 1)

                tile_step(NT + 3, 1, SV, True, False)
                with dve.Fori(NT // 2 + 2, NT) as i2:
                    for s in range(2):
                        tile_step(2 * i2 + s, s, SV, True, False)
                take_out(2 * NT - 2, 0, True)
                for s in range(HP):
                    less_mean(dve, nc, t, 0, s)
                    times_rstd(dve, nc, t, 0, s)
                for s in range(HP):
                    low_h(dve, nc, t, 0, s)
                take_out(2 * NT - 1, 1, True)

            @block.gpsimd
            def _(pool):
                nc.gpsimd.memset(t.ident32[:, :], 0.0).then_inc(zero_set, 1)
                pool.wait_ge(zero_set, 1)
                nc.gpsimd.affine_select(out=t.ident32[:, :], in_=t.ident32[:, :], compare_op=ALU.not_equal, fill=1.0,
                                        base=0, pattern=[[-1, P]], channel_multiplier=1).then_inc(zero_set, 1)
                pool.wait_ge(zero_set, 2)
                nc.gpsimd.memset(t.ones[:, :], 1.0).then_inc(flat_free, 2)

                def maxima(n, lo, hi):
                    pool.wait_ge(part_ready, n)
                    nc.gpsimd.partition_all_reduce(whole[:, lo:hi], part[:, lo:hi], P, ABSMAX).then_inc(whole_max, 1)

                maxima(1, OF_G, OF_K)
                maxima(2, OF_K, OF_M)

                def lo_out(i, value):
                    for o in range(KC):
                        pool.wait_ge(out_hi, KC * i + o + 1)
                        if value:
                            hi = t.v[:, bass.ds((i - NT) * (KC * D) + o * D, D)]
                            lo = t.v[:, bass.ds((i - NT) * (KC * D) + o * D + D * N // P, D)]
                        else:
                            hi = t.w[:, bass.ds(i * TILE + o * N, TILE)]
                            lo = t.w[:, bass.ds(i * TILE + (KC + o) * N, TILE)]
                        nc.gpsimd.tensor_tensor(lo, flat[:, o % 2, :], hi, ALU.subtract).then_inc(flat_free, 1)

                with pool.Fori(0, NT - 3) as i:
                    lo_out(i, False)
                maxima(3, OF_M, OF_V + 1)
                with pool.Fori(NT - 3, NT) as i:
                    lo_out(i, False)
                with pool.Fori(NT, 2 * NT) as i:
                    lo_out(i, True)


def h_piece(t, k, a, s):
    n = KC * NB // HP
    flat = t.hT[:, bass.ds((k % 2) * (2 * KC * NB) + a * (KC * NB) + s * n, n)]
    return flat.rearrange("p (c n) -> p c n", c=KC // HP)


def x_piece(t, s):
    return t.x_ln[:, s * (KC // HP):(s + 1) * (KC // HP), :]


def load_h_inputs(sp, t, x_cols, row_stats, k):
    sp.dma_start(t.x_ln[:, :, :].rearrange("p c n -> p (c n)"), x_cols[bass.ts(k, P), :]).then_inc(t.xln_in, 16)
    sp.dma_start(t.stats_rows[:, :, :], row_stats[:, bass.ts(k, NB)].partition_broadcast(P)).then_inc(t.xln_in, 16)


def less_mean(dve, nc, t, k, s):
    if s == 0:
        dve.wait_ge(t.xln_in, 32 * (k + 1))
    rows = t.stats_rows[:, 0:1, :].to_broadcast([P, KC // HP, NB])
    nc.vector.tensor_tensor(x_piece(t, s), x_piece(t, s), rows, ALU.subtract).then_inc(t.centred, 1)


def times_rstd(dve, nc, t, k, s):
    dve.wait_ge(t.centred, HP * k + s + 1)
    rows = t.stats_rows[:, 1:2, :].to_broadcast([P, KC // HP, NB])
    nc.vector.tensor_tensor(x_piece(t, s), x_piece(t, s), rows, ALU.mult).then_inc(t.normed, 1)


def high_h(act, nc, t, k, s):
    act.wait_ge(t.normed, HP * k + s + 1)
    nc.scalar.activation(h_piece(t, k, 0, s), x_piece(t, s), ACT.Relu).then_inc(t.h_hi, 1)


def low_h(dve, nc, t, k, s):
    dve.wait_ge(t.h_hi, HP * k + s + 1)
    nc.vector.scalar_tensor_tensor(out=h_piece(t, k, 1, s), in0=x_piece(t, s), scalar=0.0, in1=h_piece(t, k, 0, s),
                                   op0=ALU.max, op1=ALU.subtract).then_inc(t.h_lo, 1)


def attend(nc, t, x, x_cols, row_stats, adj_steps, out):
    with ExitStack() as ctx:
        sb = lambda name, shape, dt: ctx.enter_context(nc.sbuf_tensor(name, shape, dt))
        sem = lambda name: ctx.enter_context(nc.semaphore(name))

        ring = sb("ring", [P, RING * STEP], F32)
        adj = sb("adj", [P, 2, STEP], F32)
        mask = sb("mask", [P, STEP], F32)
        ph = sb("ph", [P, 2, 2, STEP], F16)
        col_max = sb("col_max", [P, STEP], F32)
        col_sum = sb("col_sum", [P, STEP], F32)
        x_out = sb("x_out", [P, NS, D], F32)
        max_n = sb("max_n", [P, NS], F32)
        rsum = sb("rsum", [P, NS], F32)

        scores, acc, last_acc = t.banks[2:4], t.banks[4:6], t.banks[0:2]
        max_bank = t.banks[6][:, 0:NB]
        row_bank = t.banks[7]

        adj_in = [sem(f"adj_in{s}") for s in range(2)]
        xout_in, xout_biased, stored = sem("xout_in"), sem("xout_biased"), sem("stored")
        scores_ready = sem("scores_ready")
        scored = sem("scored")
        magnitude = sem("magnitude")
        mask_ready = sem("mask_ready")
        penalised = sem("penalised")
        maxed = sem("maxed")
        max_folded = sem("max_folded")
        max_turned = sem("max_turned")
        max_found = sem("max_found")
        max_spread = sem("max_spread")
        shifted = sem("shifted")
        exped = sem("exped")
        p_hi, p_lo = sem("p_hi"), sem("p_lo")
        summed = sem("summed")
        multiplied = sem("multiplied")
        sums_folded = sem("sums_folded")
        rows_summed = sem("rows_summed")
        sum_inv, sum_scaled = sem("sum_inv"), sem("sum_scaled")
        rows_out = sem("rows_out")

        acc_of = lambda j: last_acc if isinstance(j, int) and j == BLOCKS - 1 else acc
        ring_slot = lambda g: ring[:, bass.ts(g % RING, STEP)]
        halves = lambda a: a.rearrange("p (c n) -> p c n", c=CH)

        with nc.Block() as block:

            @block.sync
            def _(sp):
                def load_adj(j, p, s):
                    g = STEPS * j + p
                    after(sp, scored, g - 1)
                    sp.dma_start(adj[:, s, :], adj_steps[bass.ts(g, P), :]).then_inc(adj_in[s], 16)

                def load_x(buf, j, done):
                    sp.dma_start(buf[:, :, :], x[bass.ts(j, NB), :].rearrange("(s p) d -> p s d", p=P)).then_inc(done, 16)

                def store(j):
                    sp.wait_ge(rows_out, j + 1)
                    sp.dma_start(out[bass.ts(j, NB), :].rearrange("(s p) d -> p s d", p=P), x_out[:, :, :]).then_inc(stored, 16)

                def iteration(j):
                    first, second = isinstance(j, int) and j == 0, isinstance(j, int) and j == 1
                    for p in range(4):
                        load_adj(j, p, p % 2)
                    if not (first or second):
                        store(j - 2)
                    with sp.Fori(2, STEPS // 2) as q:
                        for s in range(2):
                            load_adj(j, 2 * q + s, s)
                    if not first:
                        if not second:
                            sp.wait_ge(stored, 16 * (j - 1))
                        load_x(x_out, j - 1, xout_in)
                    if not (isinstance(j, int) and j + 2 >= BLOCKS):
                        sp.wait_ge(t.h_lo, HP * (j + 2))
                        load_h_inputs(sp, t, x_cols, row_stats, j + 2)

                sp.wait_ge(t.h_lo, HP)
                load_h_inputs(sp, t, x_cols, row_stats, 1)
                iteration(0)
                iteration(1)
                with sp.Fori(2, BLOCKS - 2) as j:
                    iteration(j)
                iteration(BLOCKS - 2)
                iteration(BLOCKS - 1)
                store(BLOCKS - 2)
                sp.wait_ge(stored, 16 * (BLOCKS - 1))
                load_x(x_out, BLOCKS - 1, xout_in)
                store(BLOCKS - 1)
                sp.wait_ge(stored, 16 * BLOCKS)

            @block.tensor
            def _(pe):
                def score(j, p, b):
                    g = STEPS * j + p
                    if isinstance(p, int) and p == 0:
                        pe.wait_ge(t.h_hi, HP * (j + 1))
                        pe.wait_ge(t.h_lo, HP * (j + 1))
                    after(pe, scored, g - 1)
                    for c in range(CH):
                        for n, (d, (a, e)) in enumerate([(d, ab) for d in range(KC) for ab in PASSES]):
                            w = t.w[:, bass.ds((a * KC + d) * N + c * P + p * (CH * P), P)]
                            h = t.hT[:, bass.ds((j % 2) * (2 * KC * NB) + (e * KC + d) * NB, NB)]
                            last = nc.tensor.matmul(scores[b][:, c * NB:(c + 1) * NB], w, h,
                                                    start=(n == 0), stop=(n == 3 * KC - 1))
                    last.then_inc(scores_ready, 1)

                def times_v(j, p, b):
                    g = STEPS * j + p
                    first, final = isinstance(p, int) and p == 0, isinstance(p, int) and p == STEPS - 1
                    pe.wait_ge(p_hi, g + 1)
                    pe.wait_ge(p_lo, g + 1)
                    if first and not (isinstance(j, int) and j == BLOCKS - 1):
                        after(pe, rows_out, j)
                    for c in range(CH):
                        for s in range(NS):
                            for n, (a, e) in enumerate(PASSES):
                                pr = ph[:, b, a, c * NB + s * P:c * NB + (s + 1) * P]
                                v = t.v[:, bass.ds(e * (D * N // P) + c * D + p * (CH * D), D)]
                                last = nc.tensor.matmul(acc_of(j)[s][:, :], pr, v, start=first and c == 0 and n == 0,
                                                        stop=final and c == CH - 1 and n == 2)
                    last.then_inc(multiplied, 1)

                def turn_max(j):
                    pe.wait_ge(max_folded, j + 1)
                    after(pe, sum_inv, j - 1)
                    for s in range(NS):
                        last = nc.tensor.transpose(row_bank[:, s * P:(s + 1) * P], col_max[:, s * P:(s + 1) * P], t.ident32[:, :])
                    last.then_inc(max_turned, 1)

                def spread_max(j):
                    pe.wait_ge(max_found, j + 1)
                    after(pe, shifted, STEPS * j)
                    for s in range(NS):
                        last = nc.tensor.transpose(max_bank[:, s * P:(s + 1) * P], max_n[:, s:s + 1].to_broadcast([P, P]),
                                                   t.ident32[:, :])
                    last.then_inc(max_spread, 1)

                def sum_rows(j):
                    pe.wait_ge(sums_folded, j + 1)
                    pe.wait_ge(max_found, min(j + 2, BLOCKS) if isinstance(j, int) else j + 2)
                    for s in range(NS):
                        last = nc.tensor.matmul(row_bank[:, s:s + 1], col_sum[:, s * P:(s + 1) * P], t.ones[:, :])
                    last.then_inc(rows_summed, 1)

                def iteration(j):
                    fixed = isinstance(j, int)
                    score(j, 0, 0)
                    if fixed and j == 1:
                        score(1, 1, 1)
                        turn_max(0)
                        spread_max(0)
                    else:
                        if not (fixed and j == 0):
                            spread_max(j - 1)
                        if not (fixed and j < 2):
                            sum_rows(j - 2)
                        score(j, 1, 1)

                    def step(p, b):
                        score(j, p, b)
                        if not (fixed and j == 0):
                            times_v(j - 1, p - 2, b)

                    step(2, 0)
                    step(3, 1)
                    with pe.Fori(2, STEPS // 2) as q:
                        for s in range(2):
                            step(2 * q + s, s)
                    if not (fixed and j == 0):
                        times_v(j - 1, STEPS - 2, 0)
                        turn_max(j)
                        if fixed and j == BLOCKS - 1:
                            spread_max(j)
                        times_v(j - 1, STEPS - 1, 1)

                iteration(0)
                iteration(1)
                with pe.Fori(2, BLOCKS - 1) as j:
                    iteration(j)
                iteration(BLOCKS - 1)
                last_block = BLOCKS - 1
                sum_rows(last_block - 1)
                times_v(last_block, 0, 0)
                times_v(last_block, 1, 1)
                with pe.Fori(1, STEPS // 2 - 1) as q:
                    for s in range(2):
                        times_v(last_block, 2 * q + s, s)
                times_v(last_block, STEPS - 2, 0)
                sum_rows(last_block)
                times_v(last_block, STEPS - 1, 1)

            @block.vector
            def _(dve):
                def with_adj(j, p, b):
                    g = STEPS * j + p
                    slot = ring_slot(g)
                    dve.wait_ge(scores_ready, g + 1)
                    dve.wait_ge(adj_in[b], 8 * STEPS * j + 8 * (p - b) + 16)
                    for c in range(CH):
                        last = nc.vector.scalar_tensor_tensor(
                            out=slot[:, c * NB:(c + 1) * NB], in0=scores[b][:, c * NB:(c + 1) * NB],
                            scalar=t.c[:, bass.ds(CH * p + c, 1)], in1=adj[:, b, c * NB:(c + 1) * NB],
                            op0=ALU.add, op1=ALU.mult)
                    last.then_inc(scored, 1)

                def mask_scores(j, p):
                    g = STEPS * j + p
                    slot = ring_slot(g)
                    dve.wait_ge(magnitude, g + 1)
                    nc.vector.tensor_scalar(mask[:, :], mask[:, :], t.threshold[:, 0:1], t.masked[:, 0:1],
                                            ALU.is_lt, ALU.mult).then_inc(mask_ready, 1)
                    dve.wait_ge(mask_ready, g + 1)
                    nc.vector.tensor_tensor(slot, mask[:, :], slot, ALU.add).then_inc(penalised, 1)
                    dve.wait_ge(penalised, g + 1)
                    if isinstance(p, int) and p == 0:
                        after(dve, max_turned, j)
                        nc.vector.tensor_scalar(col_max[:, :], slot, 1.0, None, ALU.mult).then_inc(maxed, 1)
                    else:
                        dve.wait_ge(maxed, g)
                        nc.vector.tensor_tensor(col_max[:, :], col_max[:, :], slot, ALU.max).then_inc(maxed, 1)

                def shift(j, p):
                    g = STEPS * j + p
                    slot = halves(ring_slot(g))
                    if isinstance(p, int) and p == 0:
                        dve.wait_ge(max_spread, j + 1)
                    nc.vector.tensor_tensor(slot, slot, max_bank[:, :].unsqueeze(1).to_broadcast([P, CH, NB]),
                                            ALU.subtract).then_inc(shifted, 1)

                def low_half(j, p, b):
                    g = STEPS * j + p
                    dve.wait_ge(p_hi, g + 1)
                    nc.vector.tensor_tensor(ph[:, b, 1, :], t.p[:, b, :], ph[:, b, 0, :], ALU.subtract).then_inc(p_lo, 1)

                def fold_max(j):
                    dve.wait_ge(maxed, STEPS * (j + 1))
                    nc.vector.tensor_tensor(col_max[:, 0:NB], col_max[:, 0:NB], col_max[:, NB:2 * NB], ALU.max).then_inc(max_folded, 1)

                def find_max(j):
                    dve.wait_ge(max_turned, j + 1)
                    nc.vector.tensor_reduce(max_n[:, :], row_bank[:, 0:NB].rearrange("p (s k) -> p s k", s=NS),
                                            AX.X, ALU.max).then_inc(max_found, 1)

                def rows_to_output(j):
                    dve.wait_ge(rows_summed, j + 1)
                    nc.vector.reciprocal(rsum[:, :], row_bank[:, 0:NS]).then_inc(sum_inv, 1)
                    dve.wait_ge(sum_inv, j + 1)
                    nc.vector.tensor_scalar(rsum[:, :], rsum[:, :], t.inv_sigma_v[:, 0:1], None, ALU.mult).then_inc(sum_scaled, 1)
                    dve.wait_ge(sum_scaled, j + 1)
                    dve.wait_ge(multiplied, STEPS * (j + 1))
                    dve.wait_ge(xout_biased, j + 1)
                    for s in range(NS):
                        last = nc.vector.scalar_tensor_tensor(out=x_out[:, s, :], in0=acc_of(j)[s][:, :], scalar=rsum[:, s:s + 1],
                                                              in1=x_out[:, s, :], op0=ALU.mult, op1=ALU.add)
                    last.then_inc(rows_out, 1)

                def both(j, p, b):
                    with_adj(j, p, b)
                    shift(j - 1, p)
                    mask_scores(j, p)
                    if isinstance(p, int) and p == STEPS - 1:
                        fold_max(j)
                    low_half(j - 1, p, b)
                    if isinstance(j, int) and j == BLOCKS - 1 and isinstance(p, int) and p == STEPS - 1:
                        find_max(j)

                def iteration(j):
                    fixed = isinstance(j, int)
                    before = not (fixed and j == 0)
                    more = not (fixed and j == BLOCKS - 1)
                    if before:
                        if fixed and j == 1:
                            with_adj(j, 0, 0)
                            find_max(j - 1)
                        else:
                            find_max(j - 1)
                            with_adj(j, 0, 0)
                        shift(j - 1, 0)
                        if not (fixed and j < 2):
                            rows_to_output(j - 2)
                        with_adj(j, 1, 1)
                        shift(j - 1, 1)
                        low_half(j - 1, 0, 0)
                        mask_scores(j, 0)
                        low_half(j - 1, 1, 1)
                        mask_scores(j, 1)
                    else:
                        with_adj(j, 0, 0)
                        with_adj(j, 1, 1)
                        mask_scores(j, 0)

                    def step(p, b):
                        if before:
                            both(j, p, b)
                        else:
                            with_adj(j, p, b)
                            mask_scores(j, p - 1)

                    def pairs(lo, hi):
                        with dve.Fori(lo, hi) as q:
                            step(2 * q, 0)
                            step(2 * q + 1, 1)

                    pairs(1, 2)
                    if more:
                        less_mean(dve, nc, t, j + 1, 0)
                    step(4, 0)
                    if more:
                        times_rstd(dve, nc, t, j + 1, 0)
                    step(5, 1)
                    if more:
                        less_mean(dve, nc, t, j + 1, 1)
                    step(6, 0)
                    if more:
                        times_rstd(dve, nc, t, j + 1, 1)
                    step(7, 1)
                    if more:
                        low_h(dve, nc, t, j + 1, 0)
                    step(8, 0)
                    if more:
                        low_h(dve, nc, t, j + 1, 1)
                    step(9, 1)
                    pairs(5, STEPS // 2 - 1)
                    step(STEPS - 2, 0)
                    step(STEPS - 1, 1)
                    if not before:
                        mask_scores(j, STEPS - 1)
                        fold_max(j)

                iteration(0)
                iteration(1)
                with dve.Fori(2, BLOCKS - 1) as j:
                    iteration(j)
                iteration(BLOCKS - 1)
                for p in range(2):
                    shift(BLOCKS - 1, p)
                low_half(BLOCKS - 1, 0, 0)
                rows_to_output(BLOCKS - 2)
                with dve.Fori(1, STEPS // 2) as q:
                    shift(BLOCKS - 1, 2 * q)
                    low_half(BLOCKS - 1, 2 * q - 1, 1)
                    shift(BLOCKS - 1, 2 * q + 1)
                    low_half(BLOCKS - 1, 2 * q, 0)
                low_half(BLOCKS - 1, STEPS - 1, 1)
                rows_to_output(BLOCKS - 1)

            @block.scalar
            def _(act):
                def exps(j, p, b):
                    g = STEPS * j + p
                    act.wait_ge(shifted, g + 1)
                    after(act, p_lo, g - 1)
                    after(act, summed, g - 1)
                    nc.scalar.activation(t.p[:, b, :], ring_slot(g), ACT.Exp, bias=t.log_top[:, 0:1],
                                         scale=t.inv_kappa[:, 0:1]).then_inc(exped, 1)
                    act.wait_ge(exped, g + 1)
                    after(act, multiplied, g - 1)
                    nc.scalar.activation(ph[:, b, 0, :], t.p[:, b, :], ACT.Copy).then_inc(p_hi, 1)

                def magnitudes(j, p):
                    g = STEPS * j + p
                    act.wait_ge(scored, g + 1)
                    after(act, mask_ready, g)
                    after(act, penalised, g)
                    nc.scalar.activation(mask[:, :], ring_slot(g), ACT.Abs).then_inc(magnitude, 1)

                def iteration(j):
                    fixed = isinstance(j, int)
                    before = not (fixed and j == 0)
                    more = not (fixed and j == BLOCKS - 1)

                    def step(p, b):
                        if not before:
                            magnitudes(j, p)
                        elif isinstance(p, int) and p < 2:
                            exps(j - 1, p, b)
                            magnitudes(j, p)
                        else:
                            magnitudes(j, p)
                            exps(j - 1, p, b)

                    def pairs(lo, hi):
                        with act.Fori(lo, hi) as q:
                            step(2 * q, 0)
                            step(2 * q + 1, 1)

                    for p in range(2):
                        step(p, p)
                    pairs(1, 3)
                    step(6, 0)
                    if more:
                        if not (fixed and j == 0):
                            act.wait_ge(scores_ready, STEPS * j)
                        high_h(act, nc, t, j + 1, 0)
                    step(7, 1)
                    if more:
                        high_h(act, nc, t, j + 1, 1)
                    pairs(4, STEPS // 2)

                iteration(0)
                iteration(1)
                with act.Fori(2, BLOCKS - 1) as j:
                    iteration(j)
                iteration(BLOCKS - 1)
                with act.Fori(0, STEPS // 2) as q:
                    for s in range(2):
                        exps(BLOCKS - 1, 2 * q + s, s)

            @block.gpsimd
            def _(pool):
                def add_up(j, p, b):
                    g = STEPS * j + p
                    pool.wait_ge(exped, g + 1)
                    if isinstance(p, int) and p == 1:
                        after(pool, rows_summed, j)
                        nc.gpsimd.tensor_tensor(col_sum[:, :], t.p[:, 0, :], t.p[:, 1, :], ALU.add).then_inc(summed, 2)
                    else:
                        pool.wait_ge(summed, g)
                        nc.gpsimd.tensor_tensor(col_sum[:, :], col_sum[:, :], t.p[:, b, :], ALU.add).then_inc(summed, 1)

                def block_sums(j):
                    add_up(j, 1, 1)
                    with pool.Fori(1, STEPS // 2) as q:
                        for s in range(2):
                            add_up(j, 2 * q + s, s)
                    pool.wait_ge(summed, STEPS * (j + 1))
                    nc.gpsimd.tensor_tensor(col_sum[:, 0:NB], col_sum[:, 0:NB], col_sum[:, NB:2 * NB], ALU.add).then_inc(sums_folded, 1)
                    pool.wait_ge(xout_in, 16 * (j + 1))
                    for s in range(NS):
                        last = nc.gpsimd.tensor_tensor(x_out[:, s, :], x_out[:, s, :], t.out_bias[:, :], ALU.add)
                    last.then_inc(xout_biased, 1)

                block_sums(0)
                with pool.Fori(1, BLOCKS) as j:
                    block_sums(j)


class Kept:
    pass


def build(nc, x, x_cols, adj_steps, kv_rows, kv_cols, wq, wk, wv, wmT, bq, bk, bv, bm, out):
    with ExitStack() as ctx:
        sb = lambda name, shape, dt: ctx.enter_context(nc.sbuf_tensor(name, shape, dt))
        t = Kept()
        t.w = sb("w", [P, 2 * KC * N], F16)
        t.v = sb("v", [P, 2 * (N // P) * D], F16)
        t.p = sb("p", [P, 2, STEP], F32)
        t.out_bias = sb("out_bias", [P, D], F32)
        t.ident32 = sb("ident32", [P, P], F32)
        t.ones = sb("ones", [P, 1], F32)
        t.x_ln = sb("x_ln", [P, KC, NB], F32)
        t.stats_rows = sb("stats_rows", [P, 2, NB], F32)
        t.hT = sb("hT", [P, 2 * 2 * KC * NB], F16)
        t.banks = [ctx.enter_context(nc.psum_tensor(f"bank{i}", [P, 512], F32)) for i in range(8)]
        t.xln_in, t.centred, t.normed, t.h_hi, t.h_lo = (
            ctx.enter_context(nc.semaphore(s)) for s in ("xln_in", "centred", "normed", "h_hi", "h_lo"))
        t.c = sb("c", [P, N // P], F32)
        column = lambda name: sb(name, [P, 1], F32)
        t.inv_kappa, t.threshold, t.masked = column("inv_kappa"), column("threshold"), column("masked")
        t.log_top, t.inv_sigma_v = column("log_top"), column("inv_sigma_v")
        row_stats = nc.dram_tensor("row_stats", (2, N), F32, kind="Internal").ap()
        fold_and_project(nc, t, x, x_cols, row_stats, kv_rows, kv_cols, wq, wk, wv, wmT, bq, bk, bv, bm)
        attend(nc, t, x, x_cols, row_stats, adj_steps, out)


def kernel(x, adj, L0_gnn_key, L0_gnn_value, L0_gnn_Wq, L0_gnn_bq, L0_gnn_Wk, L0_gnn_bk, L0_gnn_Wv, L0_gnn_bv,
           L0_gnn_Wm, L0_gnn_bm):
    import numpy as np
    import concourse.bacc as bacc
    from concourse import mybir as mb
    from concourse.bass_utils import run_bass_kernel_spmd

    adj = np.asarray(adj)
    kv = np.concatenate([np.asarray(L0_gnn_key), np.asarray(L0_gnn_value)], axis=0)
    steps = adj.reshape(BLOCKS, NB, STEPS, CH, P).transpose(0, 2, 4, 3, 1).reshape(BLOCKS * STEPS * P, STEP)
    x_cols = np.asarray(x).reshape(BLOCKS, NB, KC, P).transpose(0, 3, 2, 1).reshape(BLOCKS * P, KC * NB)
    arrays = {
        "x": x, "x_cols": x_cols, "adj_steps": steps, "kv_rows": kv, "kv_cols": kv.T, "wq": L0_gnn_Wq, "wk": L0_gnn_Wk,
        "wv": L0_gnn_Wv, "wmT": np.asarray(L0_gnn_Wm).T, "bq": L0_gnn_bq, "bk": L0_gnn_bk, "bv": L0_gnn_bv, "bm": L0_gnn_bm,
    }
    arrays = {k: np.ascontiguousarray(a) for k, a in arrays.items()}
    nc = bacc.Bacc("TRN2", target_bir_lowering=False, num_devices=1)
    args = [nc.dram_tensor(k, a.shape, mb.dt.from_np(a.dtype), kind="ExternalInput").ap() for k, a in arrays.items()]
    args.append(nc.dram_tensor("out", (N, D), mb.dt.from_np(np.dtype("float32")), kind="ExternalOutput").ap())
    build(nc, *args)
    r = run_bass_kernel_spmd(nc, [arrays], core_ids=[0])
    return r.results[0]["out"]
```
